# Optimizing a Trainium2 kernel written in Bass

```python
import numpy as np
import jax
import jax.numpy as jnp

def _softmax(x, axis=-1):
    return jax.nn.softmax(x, axis=axis)

def _gelu(x):
    return jax.nn.gelu(x, approximate=True)

def _silu(x):
    return jax.nn.silu(x)

def _sigmoid(x):
    return jax.nn.sigmoid(x)

def _layernorm(x, axis=-1, eps=1e-05):
    m = jnp.mean(x, axis=axis, keepdims=True)
    v = jnp.var(x, axis=axis, keepdims=True)
    return (x - m) / jnp.sqrt(v + eps)

def _scatter_add(tgt, idx, src, axis=0):
    return tgt.at[idx].add(src)

def _segment_sum(src, seg, n):
    return jax.ops.segment_sum(src, seg, n)
kernel_name = 'mk_decoder_preln_d1_seqx_r4_8ecb85'

def setup_inputs(seed: int=0):
    np.random.seed(seed)
    _w = jnp.asarray

    def _rec_inputs():
        import jax
        import jax.numpy as jnp
        _rk = jax.random.key(seed)
        x = -0.0002928 + 1 * jax.random.normal(jax.random.fold_in(_rk, 1), (128, 128, 256), jnp.float32)
        _lenS = 128 - jax.random.randint(jax.random.fold_in(_rk, 7), (128,), 0, max(1, 128 // 4) + 1, jnp.int32)
        _lenS2 = 128 - jax.random.randint(jax.random.fold_in(_rk, 8), (128,), 0, max(1, 128 // 4) + 1, jnp.int32)
        _ctx_1024P = jax.random.normal(jax.random.fold_in(_rk, 11), (128, 16, 256), jnp.float32)
        _ctx_1024c = jax.random.dirichlet(jax.random.fold_in(_rk, 511), 0.3 * jnp.ones((16,), jnp.float32), (128, 128))
        _ctx_1024t = jnp.einsum('bsk,bkd->bsd', _ctx_1024c, _ctx_1024P)
        _ctx_1024t = _ctx_1024t * jax.lax.rsqrt(jnp.mean(jnp.square(_ctx_1024t)) + 1e-12) * 0.953939
        ctx_1024 = -1.39393e-06 + 0.999914 * (_ctx_1024t + 0.3 * jax.random.normal(jax.random.fold_in(_rk, 611), (128, 128, 256), jnp.float32))
        return (x, ctx_1024)
    x, ctx_1024 = _rec_inputs()

    def _L0_attn_setup():
        import jax, jax.numpy as jnp
        import numpy as np
        D_MODEL = 256
        N_HEADS = 16
        HEAD_DIM = D_MODEL // N_HEADS
        KV_LATENT = 64
        LN_EPS = 1e-05

        def apply_rope(x):
            b, h, t, d = x.shape
            half = d // 2
            pos = jnp.arange(t, dtype=x.dtype)[:, None]
            inv_freq = 1.0 / 10000.0 ** (jnp.arange(half, dtype=x.dtype) / half)
            angles = pos * inv_freq[None, :]
            sin = jnp.sin(angles)[None, None]
            cos = jnp.cos(angles)[None, None]
            x1, x2 = (x[..., :half], x[..., half:])
            return jnp.concatenate([x1 * cos - x2 * sin, x1 * sin + x2 * cos], axis=-1)
        key = jax.random.key(seed)
        ks = jax.random.split(key, 6)
        d, L = (D_MODEL, KV_LATENT)
        s = 1.0 / np.sqrt(d)
        sl = 1.0 / np.sqrt(L)
        return {'x': jax.random.normal(ks[0], (2, 512, d), dtype=jnp.float32), 'W_q': jax.random.uniform(ks[1], (d, d), jnp.float32, -s, s), 'W_dkv': jax.random.uniform(ks[2], (d, L), jnp.float32, -s, s), 'W_uk': jax.random.uniform(ks[3], (L, d), jnp.float32, -sl, sl), 'W_uv': jax.random.uniform(ks[4], (L, d), jnp.float32, -sl, sl), 'W_o': jax.random.uniform(ks[5], (d, d), jnp.float32, -s, s), 'ln_gamma': jnp.ones((L,), jnp.float32), 'ln_beta': jnp.zeros((L,), jnp.float32)}
    _L0_attn_all = _L0_attn_setup()
    _L0_attn_in = {k: v for k, v in _L0_attn_all.items() if k in ('W_q', 'W_dkv', 'W_uk', 'W_uv', 'W_o', 'ln_gamma', 'ln_beta')}
    del _L0_attn_all

    def _L0_xattn_setup():
        import jax, jax.numpy as jnp
        import numpy as np
        HEAD_NUM = 16
        D_MODEL = 256
        B, S = (2, 512)

        def _split_heads(x):
            b, s, _ = x.shape
            return x.reshape(b, s, HEAD_NUM, D_MODEL // HEAD_NUM).transpose(0, 2, 1, 3)
        key = jax.random.key(seed)
        ks = jax.random.split(key, 12)
        scale = 1.0 / np.sqrt(D_MODEL)
        inp = {'query': jax.random.normal(ks[0], (B, S, D_MODEL), dtype=jnp.float32), 'key_in': jax.random.normal(ks[1], (B, S, D_MODEL), dtype=jnp.float32), 'value': jax.random.normal(ks[2], (B, S, D_MODEL), dtype=jnp.float32)}
        for i, name in enumerate(['w1', 'w2', 'w3', 'w4']):
            inp[name] = jax.random.normal(ks[3 + i], (D_MODEL, D_MODEL), dtype=jnp.float32) * scale
        for i, name in enumerate(['b1', 'b2', 'b3', 'b4']):
            inp[name] = jax.random.normal(ks[7 + i], (D_MODEL,), dtype=jnp.float32) * 0.01
        return inp
    _L0_xattn_all = _L0_xattn_setup()
    _L0_xattn_in = {k: v for k, v in _L0_xattn_all.items() if k in ('w1', 'w2', 'w3', 'w4', 'b1', 'b2', 'b3', 'b4')}
    del _L0_xattn_all

    def _L0_ffn_setup():
        import jax, jax.numpy as jnp
        import numpy as np
        TOP_K = 2
        NUM_EXPERTS = 8
        key = jax.random.key(seed)
        ks = jax.random.split(key, 8)
        h, d, ds, E = (256, 128, 256, NUM_EXPERTS)
        s = 1.0 / np.sqrt(h)
        return {'x': jax.random.normal(ks[0], (2, 512, h), jnp.float32), 'router': jax.random.normal(ks[1], (h, E), jnp.float32) * s, 'experts_gate': jax.random.normal(ks[2], (E, h, d), jnp.float32) * s, 'experts_up': jax.random.normal(ks[3], (E, h, d), jnp.float32) * s, 'experts_down': jax.random.normal(ks[4], (E, d, h), jnp.float32) * (1.0 / np.sqrt(d)), 'shared_gate': jax.random.normal(ks[5], (h, ds), jnp.float32) * s, 'shared_up': jax.random.normal(ks[6], (h, ds), jnp.float32) * s, 'shared_down': jax.random.normal(ks[7], (ds, h), jnp.float32) * (1.0 / np.sqrt(ds))}
    _L0_ffn_all = _L0_ffn_setup()
    _L0_ffn_in = {k: v for k, v in _L0_ffn_all.items() if k in ('router', 'experts_gate', 'experts_up', 'experts_down', 'shared_gate', 'shared_up', 'shared_down')}
    del _L0_ffn_all
    return {'x': x, 'ctx_1024': ctx_1024, 'L0_attn_W_q': _L0_attn_in['W_q'], 'L0_attn_W_dkv': _L0_attn_in['W_dkv'], 'L0_attn_W_uk': _L0_attn_in['W_uk'], 'L0_attn_W_uv': _L0_attn_in['W_uv'], 'L0_attn_W_o': _L0_attn_in['W_o'], 'L0_attn_ln_gamma': _L0_attn_in['ln_gamma'], 'L0_attn_ln_beta': _L0_attn_in['ln_beta'], 'L0_xattn_w1': _L0_xattn_in['w1'], 'L0_xattn_w2': _L0_xattn_in['w2'], 'L0_xattn_w3': _L0_xattn_in['w3'], 'L0_xattn_w4': _L0_xattn_in['w4'], 'L0_xattn_b1': _L0_xattn_in['b1'], 'L0_xattn_b2': _L0_xattn_in['b2'], 'L0_xattn_b3': _L0_xattn_in['b3'], 'L0_xattn_b4': _L0_xattn_in['b4'], 'L0_ffn_router': _L0_ffn_in['router'], 'L0_ffn_experts_gate': _L0_ffn_in['experts_gate'], 'L0_ffn_experts_up': _L0_ffn_in['experts_up'], 'L0_ffn_experts_down': _L0_ffn_in['experts_down'], 'L0_ffn_shared_gate': _L0_ffn_in['shared_gate'], 'L0_ffn_shared_up': _L0_ffn_in['shared_up'], 'L0_ffn_shared_down': _L0_ffn_in['shared_down']}

def reference(x, ctx_1024, L0_attn_W_q, L0_attn_W_dkv, L0_attn_W_uk, L0_attn_W_uv, L0_attn_W_o, L0_attn_ln_gamma, L0_attn_ln_beta, L0_xattn_w1, L0_xattn_w2, L0_xattn_w3, L0_xattn_w4, L0_xattn_b1, L0_xattn_b2, L0_xattn_b3, L0_xattn_b4, L0_ffn_router, L0_ffn_experts_gate, L0_ffn_experts_up, L0_ffn_experts_down, L0_ffn_shared_gate, L0_ffn_shared_up, L0_ffn_shared_down):
    import jax
    import jax.numpy as jnp

    def _L0_attn_ref(x, W_q, W_dkv, W_uk, W_uv, W_o, ln_gamma, ln_beta):
        import jax, jax.numpy as jnp
        import numpy as np
        D_MODEL = 256
        N_HEADS = 16
        HEAD_DIM = D_MODEL // N_HEADS
        KV_LATENT = 64
        LN_EPS = 1e-05

        def apply_rope(x):
            b, h, t, d = x.shape
            half = d // 2
            pos = jnp.arange(t, dtype=x.dtype)[:, None]
            inv_freq = 1.0 / 10000.0 ** (jnp.arange(half, dtype=x.dtype) / half)
            angles = pos * inv_freq[None, :]
            sin = jnp.sin(angles)[None, None]
            cos = jnp.cos(angles)[None, None]
            x1, x2 = (x[..., :half], x[..., half:])
            return jnp.concatenate([x1 * cos - x2 * sin, x1 * sin + x2 * cos], axis=-1)
        b, t, _ = x.shape
        q = (x @ W_q).reshape(b, t, N_HEADS, HEAD_DIM).transpose(0, 2, 1, 3)
        lat = x @ W_dkv
        mu = jnp.mean(lat, axis=-1, keepdims=True)
        var = jnp.mean(jnp.square(lat - mu), axis=-1, keepdims=True)
        lat = (lat - mu) * jax.lax.rsqrt(var + LN_EPS) * ln_gamma + ln_beta
        k = (lat @ W_uk).reshape(b, t, N_HEADS, HEAD_DIM).transpose(0, 2, 1, 3)
        v = (lat @ W_uv).reshape(b, t, N_HEADS, HEAD_DIM).transpose(0, 2, 1, 3)
        q = apply_rope(q)
        k = apply_rope(k)
        scores = jnp.einsum('bhqd,bhkd->bhqk', q, k) / jnp.sqrt(jnp.float32(HEAD_DIM))
        causal = jnp.tril(jnp.ones((t, t), dtype=bool))
        scores = jnp.where(causal[None, None], scores, -jnp.inf)
        attn = jax.nn.softmax(scores, axis=-1)
        out = jnp.einsum('bhqk,bhkd->bhqd', attn, v)
        out = out.transpose(0, 2, 1, 3).reshape(b, t, D_MODEL)
        return out @ W_o

    def _L0_xattn_ref(query, key_in, value, w1, w2, w3, w4, b1, b2, b3, b4):
        import jax, jax.numpy as jnp
        import numpy as np
        HEAD_NUM = 16
        D_MODEL = 256
        B, S = (2, 512)

        def _split_heads(x):
            b, s, _ = x.shape
            return x.reshape(b, s, HEAD_NUM, D_MODEL // HEAD_NUM).transpose(0, 2, 1, 3)
        d_k = D_MODEL // HEAD_NUM
        q = _split_heads(query @ w1.T + b1)
        k = _split_heads(key_in @ w2.T + b2)
        v = _split_heads(value @ w3.T + b3)
        scores = jnp.einsum('bhqd,bhkd->bhqk', q, k) / jnp.sqrt(jnp.float32(d_k))
        attn = jax.nn.softmax(scores, axis=-1)
        out = jnp.einsum('bhqk,bhkd->bhqd', attn, v)
        out = out.transpose(0, 2, 1, 3).reshape(query.shape[0], -1, D_MODEL)
        return out @ w4.T + b4

    def _L0_ffn_ref(x, router, experts_gate, experts_up, experts_down, shared_gate, shared_up, shared_down):
        import jax, jax.numpy as jnp
        import numpy as np
        TOP_K = 2
        NUM_EXPERTS = 8
        b, s, h = x.shape
        E = router.shape[1]
        shared_act = jax.nn.silu(jnp.einsum('bsh,hd->bsd', x, shared_gate))
        shared_up_out = jnp.einsum('bsh,hd->bsd', x, shared_up)
        shared_out = jnp.einsum('bsd,dh->bsh', shared_act * shared_up_out, shared_down)
        router_probs = jax.nn.softmax(jnp.einsum('bsh,he->bse', x, router), axis=-1)
        topk_probs, topk_idx = jax.lax.top_k(router_probs, TOP_K)
        coef = jnp.sum(jax.nn.one_hot(topk_idx, E, dtype=x.dtype) * topk_probs[..., None], axis=2)
        coef = coef.reshape(b * s, E)
        x_flat = x.reshape(b * s, h)
        gate = jnp.einsum('th,ehd->etd', x_flat, experts_gate)
        up = jnp.einsum('th,ehd->etd', x_flat, experts_up)
        expert_out = jnp.einsum('etd,edh->eth', jax.nn.silu(gate) * up, experts_down)
        routed = jnp.einsum('eth,te->th', expert_out, coef)
        return routed.reshape(b, s, h) + shared_out
    x = x + _L0_attn_ref(_layernorm(x, axis=-1), L0_attn_W_q, L0_attn_W_dkv, L0_attn_W_uk, L0_attn_W_uv, L0_attn_W_o, L0_attn_ln_gamma, L0_attn_ln_beta)
    x = x + _L0_xattn_ref(_layernorm(x, axis=-1), ctx_1024, ctx_1024, L0_xattn_w1, L0_xattn_w2, L0_xattn_w3, L0_xattn_w4, L0_xattn_b1, L0_xattn_b2, L0_xattn_b3, L0_xattn_b4)
    x = x + _L0_ffn_ref(_layernorm(x, axis=-1), L0_ffn_router, L0_ffn_experts_gate, L0_ffn_experts_up, L0_ffn_experts_down, L0_ffn_shared_gate, L0_ffn_shared_up, L0_ffn_shared_down)
    return x

_drawn_inputs = setup_inputs


def setup_inputs(seed=0):
    import zlib

    import numpy as np

    out = dict(_drawn_inputs(seed))
    spreads = {'L0_attn_ln_gamma': (1.0, 0.6), 'L0_attn_ln_beta': (0.0, 0.1)}
    factors = {'L0_xattn_b1': 8.0, 'L0_xattn_b2': 8.0, 'L0_xattn_b3': 3.751, 'L0_xattn_b4': 4.12}
    for name, (base, spread) in spreads.items():
        noise = np.random.default_rng([zlib.crc32(name.encode()), seed]).standard_normal(out[name].shape)
        drawn = base * np.exp(spread * noise) if base else spread * noise
        out[name] = jnp.asarray(drawn.astype(out[name].dtype))
    for name, factor in factors.items():
        out[name] = (out[name] * factor).astype(out[name].dtype)
    return out
```

```python
from contextlib import ExitStack

import numpy as np

import concourse.bass as bass
from concourse import mybir

F32 = mybir.dt.float32
F16 = mybir.dt.float16
BF16 = mybir.dt.bfloat16
ALU = mybir.AluOpType
ACT = mybir.ActivationFunctionType
AX_X = mybir.AxisListType.X

P = 128
BATCH, SEQ, D = 128, 128, 256
HEADS, HD = 16, 16
LATENT = 64
EXPERTS, TOP_K = 8, 2
SHARED_TILES = 2
TILES = SHARED_TILES + EXPERTS
NSEQ = 2
T = NSEQ * SEQ
NBLOCKS = BATCH // NSEQ
KT = D // P
HG = 4
GROUPS = HEADS // HG
PAIRS = HEADS // 2
VW = 32
EPS = 1e-5
WS = 16.0
SCORE_SCALE = 1.0 / (HD ** 0.5) / (WS * WS)
MASKED = -1e30

SELF_IN, SELF_OUT, CROSS_IN, CROSS_OUT, FFN = range(5)
STAGES = (SELF_IN, SELF_OUT, CROSS_IN, CROSS_OUT, FFN)
ITERATIONS = NBLOCKS + len(STAGES) - 1
LOOP_FROM = 6
LOOP_TO = NBLOCKS - 2

WIDE = {}
_at = 0
for _name, _n in (("q", D), ("q_turned", D), ("down_latent", LATENT), ("self_out", D), ("cross_q", D),
                  ("cross_k", D), ("cross_v", D), ("cross_out", D), ("shared_gate", D), ("shared_up", D),
                  ("shared_down", D), ("router", EXPERTS), ("gate", EXPERTS * P), ("up", EXPERTS * P)):
    WIDE[_name] = _at
    _at += _n
WIDE_COLS = _at
LAT = {"k": 0, "k_turned": D, "v": 2 * D}
LAT_COLS = 3 * D
CHUNK = 1024

NSLOTS = 25


def steps_of_slot(n):
    steps = []
    steps += {0: [(FFN, "norm", 0)], 1: [(FFN, "norm_turn", 0)], 2: [(FFN, "router", 0)],
              3: [(FFN, "choose", 0)]}.get(n, [])
    for stage, m in ((SELF_OUT, n), (CROSS_OUT, n)):
        if m < 16:
            seq, k = divmod(m, 8)
            steps.append((stage, "scores" if k < GROUPS else "weights", seq * GROUPS + k % GROUPS))
        for seq in range(NSEQ):
            k = m - (8 * seq + GROUPS + 1)
            if 0 <= k < GROUPS:
                steps.append((stage, "values", seq * GROUPS + k))
            if k == GROUPS:
                steps.append((stage, "turn", seq))
        if m == 19:
            steps.append((stage, "feature_turn", 0))
        if m == 21:
            steps.append((stage, "project", 0))
    steps += {0: [(SELF_IN, "norm", 0)], 1: [(SELF_IN, "norm_turn", 0)], 2: [(SELF_IN, "rotary", 0)],
              3: [(SELF_IN, "latent", 0)], 4: [(SELF_IN, "rotary", 1)], 6: [(SELF_IN, "latent_turn", 0)],
              8: [(SELF_IN, "rotary", 2)], 9: [(SELF_IN, "rotary", 3)], 10: [(SELF_IN, "latent_values", 0)],
              11: [(CROSS_IN, "norm", 0)], 12: [(CROSS_IN, "context_turn", 0)],
              13: [(CROSS_IN, "norm_turn", 0)], 14: [(CROSS_IN, "keys", 0)], 16: [(CROSS_IN, "queries", 0)],
              18: [(CROSS_IN, "context_values", 0)]}.get(n, [])
    if n >= 3 and (n - 3) % 2 == 0 and (n - 3) // 2 < TILES:
        steps.append((FFN, "hidden", (n - 3) // 2))
    if n >= 4 and (n - 4) % 2 == 0 and (n - 4) // 2 < TILES:
        steps.append((FFN, "split", (n - 4) // 2))
    if n >= 5 and (n - 5) % 2 == 0 and (n - 5) // 2 < TILES:
        steps.append((FFN, "down", (n - 5) // 2))
    if n == NSLOTS - 1:
        steps.append((FFN, "finish", 0))
    return steps


STEPS = [step for n in range(NSLOTS) for step in steps_of_slot(n)]


class Signal:

    def __init__(self, sem, stage, per_block=1, unit=1):
        self.sem, self.stage, self.per_block, self.unit = sem, stage, per_block, unit

    def at(self, i, n=None):
        n = self.per_block if n is None else n
        return ((i - self.stage) * self.per_block + n) * self.unit

    def begun(self, i, n=None):
        value = self.at(i, n)
        return not isinstance(value, int) or value > 0


def decoder_layer(nc, x, ctx, wide, expert_down, latent_weights, gamma, beta, b1, b2, b3, b4,
                  rotary_table, causal, causal_turned, out):
    ctx_stack = ExitStack()
    with ctx_stack:
        def sb(name, shape, dt):
            return ctx_stack.enter_context(nc.sbuf_tensor(name, shape, dt))

        def bank(name, shape=(P, 512)):
            return ctx_stack.enter_context(nc.psum_tensor(name, list(shape), F32))

        def sem(name):
            return ctx_stack.enter_context(nc.semaphore(name))

        def signal(name, stage, per_block=1, unit=1):
            return Signal(sem(name), stage, per_block, unit)

        wide_hi = sb("wide_hi", [P, KT, WIDE_COLS], F16)
        wide_lo = sb("wide_lo", [P, KT, WIDE_COLS], F16)
        down_hi = sb("down_hi", [P, EXPERTS * D], F16)
        down_lo = sb("down_lo", [P, EXPERTS * D], F16)
        lat_hi = sb("lat_hi", [P, LAT_COLS], F16)
        lat_lo = sb("lat_lo", [P, LAT_COLS], F16)
        gamma_sb = sb("gamma_sb", [P, 1], F32)
        gamma_scaled = sb("gamma_scaled", [P, 1], F32)
        beta_sb = sb("beta_sb", [P, 1], F32)
        b1_sb = sb("b1_sb", [P, KT], F32)
        b2_sb = sb("b2_sb", [P, KT], F32)
        b1_scaled = sb("b1_scaled", [P, KT], F32)
        b2_scaled = sb("b2_scaled", [P, KT], F32)
        b3_sb = sb("b3_sb", [P, D], F32)
        b4_sb = sb("b4_sb", [P, D], F32)
        rotary_sb = sb("rotary_sb", [P, 2, T], F32)
        causal_f32 = sb("causal_f32", [P, 2, SEQ], F32)
        causal_sb = sb("causal_sb", [P, 2, HG * SEQ], BF16)
        ident = sb("ident", [P, P], F32)
        ident16 = sb("ident16", [P, P], F16)
        ident_bf = sb("ident_bf", [P, P], BF16)
        minus_ident = sb("minus_ident", [P, P], BF16)
        earlier = sb("earlier", [P, EXPERTS, EXPERTS], F32)
        minus_half = sb("minus_half", [P, NSEQ], F32)

        NORMED = (SELF_IN, CROSS_IN, FFN)
        tag = {SELF_IN: "self", CROSS_IN: "cross", FFN: "ffn", SELF_OUT: "selfo", CROSS_OUT: "crosso"}
        stats = {z: sb(f"stats_{tag[z]}", [P, NSEQ, 6], F32) for z in NORMED}
        moments = {z: sb(f"moments_{tag[z]}", [P, NSEQ, 2], F32) for z in NORMED}
        variance = {z: sb(f"variance_{tag[z]}", [P, NSEQ], F32) for z in NORMED}
        rstd = {z: sb(f"rstd_{tag[z]}", [P, NSEQ], F32) for z in NORMED}
        normed = {z: sb(f"normed_{tag[z]}", [P, NSEQ, D], F32) for z in NORMED}
        xT_hi = {z: sb(f"xT_hi_{tag[z]}", [P, KT, T], F16) for z in NORMED}
        xT_lo = {z: sb(f"xT_lo_{tag[z]}", [P, KT, T], F16) for z in NORMED}

        wait_holder = sb("wait_holder", [P, 1], F32)

        x_in = sb("x_in", [P, NSEQ, D], F32)
        rotary_parts = sb("rotary_parts", [P, 2, T], F32)
        rotary_sum = sb("rotary_sum", [P, T], F32)
        self_qk_hi = sb("self_qk_hi", [P, 4, T], F16)
        self_qk_lo = sb("self_qk_lo", [P, 4, T], F16)
        lat_stats = sb("lat_stats", [P, NSEQ, 6], F32)
        lat_moments = sb("lat_moments", [P, NSEQ, 2], F32)
        lat_variance = sb("lat_variance", [P, NSEQ], F32)
        lat_rstd = sb("lat_rstd", [P, NSEQ], F32)
        lat_twice = sb("lat_twice", [P, NSEQ, 2, LATENT], F32)
        latT = sb("latT", [P, T], F32)
        latT_split = sb("latT_split", [P, T], F16)

        ctx_in = sb("ctx_in", [P, NSEQ, D], F32)
        ctxT_hi = sb("ctxT_hi", [P, KT, T], F16)
        ctxT_lo = sb("ctxT_lo", [P, KT, T], F16)
        cross_qk_hi = sb("cross_qk_hi", [P, 4, T], F16)
        cross_qk_lo = sb("cross_qk_lo", [P, 4, T], F16)

        ATT = (SELF_OUT, CROSS_OUT)
        q_packed = {z: [sb(f"q_packed_{tag[z]}{h}", [P, HEADS, T], F16) for h in range(2)] for z in ATT}
        k_packed = {z: [sb(f"k_packed_{tag[z]}{h}", [P, PAIRS, T], F16) for h in range(2)] for z in ATT}
        values = {z: [sb(f"values_{tag[z]}{h}", [P, NSEQ, HEADS, VW], F32) for h in range(2)] for z in ATT}
        probs = {z: sb(f"probs_{tag[z]}", [P, HEADS, SEQ], F32) for z in ATT}
        top_score = {z: sb(f"top_score_{tag[z]}", [P, NSEQ, HEADS], BF16) for z in ATT}
        outT = {z: sb(f"outT_{tag[z]}", [P, HG * SEQ], F32) for z in ATT}
        inverse = {z: sb(f"inverse_{tag[z]}", [P, HEADS], F32) for z in ATT}
        heads_out = {z: sb(f"heads_out_{tag[z]}", [P, NSEQ, D], F32) for z in ATT}
        headsT_hi = {z: sb(f"headsT_hi_{tag[z]}", [P, KT, T], F16) for z in ATT}
        headsT_lo = {z: sb(f"headsT_lo_{tag[z]}", [P, KT, T], F16) for z in ATT}
        x_again = sb("x_again", [P, NSEQ, D], F32)
        x1 = [sb(f"x1_{h}", [P, NSEQ, D], F32) for h in range(2)]
        x1_b4 = [sb(f"x1_b4_{h}", [P, NSEQ, D], F32) for h in range(2)]
        x2 = [sb(f"x2_{h}", [P, NSEQ, D], F32) for h in range(2)]

        logits = sb("logits", [P, NSEQ, EXPERTS], F32)
        top_logit = sb("top_logit", [P, NSEQ], F32)
        shifted = sb("shifted", [P, NSEQ, EXPERTS], F32)
        exps = sb("exps", [P, NSEQ, EXPERTS], F32)
        exp_sum = sb("exp_sum", [P, NSEQ], F32)
        exp_inv = sb("exp_inv", [P, NSEQ], F32)
        router_probs = sb("router_probs", [P, NSEQ, EXPERTS], F32)
        greater = sb("greater", [P, NSEQ, EXPERTS, EXPERTS], F32)
        equal = sb("equal", [P, NSEQ, EXPERTS, EXPERTS], F32)
        rank = sb("rank", [P, NSEQ, EXPERTS], F32)
        coef = sb("coef", [P, NSEQ, EXPERTS], F32)
        coef_hi = sb("coef_hi", [P, NSEQ, EXPERTS], F16)
        coef_lo = sb("coef_lo", [P, NSEQ, EXPERTS], F16)
        tanh_sb = sb("tanh_sb", [P, 2, T], F32)
        gated = sb("gated", [P, T], F32)
        hidden = sb("hidden", [P, T], F32)
        hidden_c = sb("hidden_c", [P, 2, T], F32)
        hidden_hi = sb("hidden_hi", [P, 2, T], F16)
        hidden_lo = sb("hidden_lo", [P, 2, T], F16)
        result = sb("result", [P, NSEQ, D], F32)

        setup_bank = bank("setup_bank")
        score_bank = {z: bank(f"score_bank_{tag[z]}") for z in ATT}
        out_bank = {z: bank(f"out_bank_{tag[z]}") for z in ATT}
        gate_up_bank = bank("gate_up_bank")
        coef_bank = bank("coef_bank")
        down_bank = bank("down_bank")

        scratch = {z: nc.dram_tensor(f"qk_scratch_{tag[z]}", [2, 4, P, T], F16, kind="Internal").ap()
                   for z in ATT}

        constants_loaded = sem("constants_loaded")
        chunk_loaded = [sem("chunk_loaded0"), sem("chunk_loaded1")]
        chunk_hi = sem("chunk_hi")
        chunk_lo = sem("chunk_lo")
        pool_ready = sem("pool_ready")
        ident_ready = sem("ident_ready")
        act_ready = sem("act_ready")
        dve_ready = sem("dve_ready")

        norm_steps = {z: signal(f"norm_steps_{tag[z]}", z, 3) for z in NORMED}
        rstd_done = {z: signal(f"rstd_done_{tag[z]}", z) for z in NORMED}
        norm_done = {z: signal(f"norm_done_{tag[z]}", z) for z in NORMED}
        norm_turned = {z: signal(f"norm_turned_{tag[z]}", z) for z in NORMED}
        xT_hi_done = {z: signal(f"xT_hi_done_{tag[z]}", z) for z in NORMED}
        xT_lo_done = {z: signal(f"xT_lo_done_{tag[z]}", z) for z in NORMED}

        x_loaded = signal("x_loaded", SELF_IN, 1, 16)
        rotary_projected = signal("rotary_projected", SELF_IN, 4)
        rotary_multiplied = signal("rotary_multiplied", SELF_IN, 4)
        rotary_added = signal("rotary_added", SELF_IN, 4)
        rotary_hi_done = signal("rotary_hi_done", SELF_IN, 4)
        rotary_lo_done = signal("rotary_lo_done", SELF_IN, 4)
        latent_projected = signal("latent_projected", SELF_IN)
        latent_steps = signal("latent_steps", SELF_IN, 3)
        latent_rstd = signal("latent_rstd", SELF_IN)
        latent_normed = signal("latent_normed", SELF_IN)
        latent_turned = signal("latent_turned", SELF_IN)
        latent_affine = signal("latent_affine", SELF_IN)
        latent_hi_done = signal("latent_hi_done", SELF_IN)
        latent_split = signal("latent_split", SELF_IN)
        values_projected = {SELF_OUT: signal("self_values_projected", SELF_IN),
                            CROSS_OUT: signal("cross_values_projected", CROSS_IN)}
        values_ready = {SELF_OUT: signal("self_values_ready", SELF_IN),
                        CROSS_OUT: signal("cross_values_ready", CROSS_IN)}
        qk_stored = {SELF_OUT: signal("self_qk_stored", SELF_IN, 2, 16),
                     CROSS_OUT: signal("cross_qk_stored", CROSS_IN, 2, 16)}
        qk_packed = {SELF_OUT: signal("self_qk_packed", SELF_IN, 12, 16),
                     CROSS_OUT: signal("cross_qk_packed", CROSS_IN, 12, 16)}

        ctx_loaded = signal("ctx_loaded", CROSS_IN, 1, 16)
        ctx_turned = signal("ctx_turned", CROSS_IN)
        ctx_hi_done = signal("ctx_hi_done", CROSS_IN)
        ctx_lo_done = signal("ctx_lo_done", CROSS_IN)
        qk_projected = signal("qk_projected", CROSS_IN, 2)
        qk_hi_done = signal("qk_hi_done", CROSS_IN, 2)
        qk_lo_done = signal("qk_lo_done", CROSS_IN, 2)
        x1_b4_done = signal("x1_b4_done", CROSS_IN)

        NG = NSEQ * GROUPS
        scored = {z: signal(f"scored_{tag[z]}", z, NG) for z in ATT}
        maxed = {z: signal(f"maxed_{tag[z]}", z, NG) for z in ATT}
        weighed = {z: signal(f"weighed_{tag[z]}", z, NG) for z in ATT}
        exped = {z: signal(f"exped_{tag[z]}", z, NG) for z in ATT}
        valued = {z: signal(f"valued_{tag[z]}", z, NG) for z in ATT}
        out_copied = {z: signal(f"out_copied_{tag[z]}", z, NSEQ) for z in ATT}
        out_turned = {z: signal(f"out_turned_{tag[z]}", z, NSEQ) for z in ATT}
        inverted = {z: signal(f"inverted_{tag[z]}", z, NSEQ) for z in ATT}
        divided = {z: signal(f"divided_{tag[z]}", z, NSEQ) for z in ATT}
        heads_turned = {z: signal(f"heads_turned_{tag[z]}", z) for z in ATT}
        heads_hi_done = {z: signal(f"heads_hi_done_{tag[z]}", z) for z in ATT}
        heads_lo_done = {z: signal(f"heads_lo_done_{tag[z]}", z) for z in ATT}
        projected = {z: signal(f"projected_{tag[z]}", z) for z in ATT}
        residual_added = {z: signal(f"residual_added_{tag[z]}", z) for z in ATT}
        x_again_loaded = signal("x_again_loaded", SELF_OUT, 1, 16)

        routed = signal("routed", FFN)
        choose_steps = signal("choose_steps", FFN, 13)
        router_exped = signal("router_exped", FFN)
        gate_up_done = signal("gate_up_done", FFN, TILES)
        coef_spread = signal("coef_spread", FFN, EXPERTS)
        tanh_done = signal("tanh_done", FFN, TILES)
        gated_done = signal("gated_done", FFN, TILES)
        hidden_done = signal("hidden_done", FFN, TILES)
        hidden_scaled = signal("hidden_scaled", FFN, EXPERTS)
        hidden_hi_done = signal("hidden_hi_done", FFN, TILES)
        hidden_lo_done = signal("hidden_lo_done", FFN, TILES)
        down_done = signal("down_done", FFN, TILES)
        result_done = signal("result_done", FFN)
        result_stored = signal("result_stored", FFN, 1, 16)

        def w(name, kt, c0, n):
            a = WIDE[name] + c0
            return wide_hi[:, kt, a:a + n], wide_lo[:, kt, a:a + n]

        chunks = []
        for kt in range(KT):
            for c in range(0, WIDE_COLS, CHUNK):
                e = min(c + CHUNK, WIDE_COLS)
                chunks.append((wide[kt * P:(kt + 1) * P, c:e], wide_hi[:, kt, c:e], wide_lo[:, kt, c:e]))
        for c in range(0, EXPERTS * D, CHUNK):
            chunks.append((expert_down[:, c:c + CHUNK], down_hi[:, c:c + CHUNK], down_lo[:, c:c + CHUNK]))
        chunks.append((latent_weights, lat_hi[:, :], lat_lo[:, :]))
        staging = [probs[z][:, :, :].rearrange("p h q -> p (h q)") for z in ATT]

        NCONST = 11

        def slot_of(i_parity, stage):
            return (i_parity + stage) % 2

        def run(eng, body):
            def active(i):
                return [z for z in STAGES if 0 <= i - z < NBLOCKS]
            for i in range(LOOP_FROM):
                body(i, i % 2, active(i))
            with eng.Fori(LOOP_FROM, LOOP_TO, 2) as i:
                body(i, 0, list(STAGES))
                body(i + 1, 1, list(STAGES))
            for i in range(LOOP_TO, ITERATIONS):
                body(i, i % 2, active(i))

        block = ctx_stack.enter_context(nc.Block())

        @block.sync
        def _(sp):
            for dst, src in ((gamma_sb[:, :], gamma), (beta_sb[:, :], beta), (b1_sb[:, :], b1),
                             (b2_sb[:, :], b2), (b3_sb[:, :], b3), (b4_sb[:, :], b4),
                             (rotary_sb[:, 0, :], rotary_table[:, 0:T]),
                             (rotary_sb[:, 1, :], rotary_table[:, T:2 * T]),
                             (causal_f32[:, 0, :], causal), (causal_f32[:, 1, :], causal_turned)):
                sp.dma_start(dst, src).then_inc(constants_loaded, 16)
            for n, (src, hi, _) in enumerate(chunks):
                if n >= 2:
                    sp.wait_ge(chunk_lo, n - 1)
                sp.dma_start(staging[n % 2][:, 0:src.shape[1]], src).then_inc(chunk_loaded[n % 2], 16)
            sp.wait_ge(pool_ready, 1)

            def rows(tensor, b):
                return tensor[bass.ds(b * NSEQ, NSEQ)].rearrange("s t d -> t s d")

            def load_x(i):
                if norm_done[SELF_IN].begun(i - 1):
                    sp.wait_ge(norm_done[SELF_IN].sem, norm_done[SELF_IN].at(i - 1))
                sp.dma_start(x_in[:, :, :], rows(x, i)).then_inc(x_loaded.sem, 16)

            def load_ctx(i):
                if ctx_turned.begun(i - 1):
                    sp.wait_ge(ctx_turned.sem, ctx_turned.at(i - 1))
                sp.dma_start(ctx_in[:, :, :], rows(ctx, i - CROSS_IN)).then_inc(ctx_loaded.sem, 16)

            def pack(i, parity, z, hi, lo, hi_done, lo_done):
                half = slot_of(parity, z - 1)
                sp.wait_ge(hi_done.sem, hi_done.at(i))
                if qk_packed[z].begun(i - 1):
                    sp.wait_ge(qk_packed[z].sem, qk_packed[z].at(i - 1))
                sp.dma_start(scratch[z][0].rearrange("m p t -> p m t"), hi[:, :, :]).then_inc(qk_stored[z].sem, 16)
                sp.wait_ge(lo_done.sem, lo_done.at(i))
                sp.dma_start(scratch[z][1].rearrange("m p t -> p m t"), lo[:, :, :]).then_inc(qk_stored[z].sem, 16)
                sp.wait_ge(qk_stored[z].sem, qk_stored[z].at(i))
                if weighed[z].begun(i - 1):
                    sp.wait_ge(weighed[z].sem, weighed[z].at(i - 1))
                for c in range(4):
                    keys = scratch[z][c % 2, 2:4].rearrange("m (j r) t -> r (m j) t", r=32)
                    sp.dma_start(k_packed[z][half][32 * c:32 * c + 32, :, :], keys).then_inc(qk_packed[z].sem, 16)
                    for odd in range(2):
                        r = 32 * c + 16 * odd
                        queries = scratch[z][c // 2, 0:2].rearrange("m (j o d) t -> o d (m j) t", o=2, d=HD)[odd]
                        dst = q_packed[z][half][r:r + HD, :, :].rearrange("d (j o) t -> d o j t", o=2)[:, odd]
                        sp.dma_start(dst, queries).then_inc(qk_packed[z].sem, 16)

            def body(i, parity, active):
                if SELF_OUT in active:
                    if residual_added[SELF_OUT].begun(i - 1):
                        sp.wait_ge(residual_added[SELF_OUT].sem, residual_added[SELF_OUT].at(i - 1))
                    sp.dma_start(x_again[:, :, :], rows(x, i - SELF_OUT)).then_inc(x_again_loaded.sem, 16)
                if SELF_IN in active:
                    pack(i, parity, SELF_OUT, self_qk_hi, self_qk_lo, rotary_hi_done, rotary_lo_done)
                    if not isinstance(i, int) or i + 1 < NBLOCKS:
                        load_x(i + 1)
                if CROSS_IN in active:
                    pack(i, parity, CROSS_OUT, cross_qk_hi, cross_qk_lo, qk_hi_done, qk_lo_done)
                if not isinstance(i, int) or 0 <= i + 1 - CROSS_IN < NBLOCKS:
                    load_ctx(i + 1)
                if FFN in active:
                    sp.wait_ge(result_done.sem, result_done.at(i))
                    sp.dma_start(rows(out, i - FFN), result[:, :, :]).then_inc(result_stored.sem, 16)

            load_x(0)
            run(sp, body)
            sp.wait_ge(result_stored.sem, result_stored.at(ITERATIONS - 1))
            sp.wait_ge(qk_packed[SELF_OUT].sem, qk_packed[SELF_OUT].at(NBLOCKS - 1 + SELF_IN))
            sp.wait_ge(qk_packed[CROSS_OUT].sem, qk_packed[CROSS_OUT].at(NBLOCKS - 1 + CROSS_IN))

        @block.gpsimd
        def _(pool):
            nc.gpsimd.memset(ident[:, :], 0.0)
            nc.gpsimd.memset(earlier[:, :, :], 1.0)
            nc.gpsimd.memset(minus_half[:, :], -0.5)
            for z in ATT:
                for half in range(2):
                    nc.gpsimd.memset(q_packed[z][half][:, :, :].bitcast(F32), 0.0)
                    last = nc.gpsimd.memset(values[z][half][:, :, :, :], 1.0)
            last.then_inc(ident_ready, 1)
            pool.wait_ge(ident_ready, 1)
            nc.gpsimd.affine_select(out=ident[:, :], in_=ident[:, :], compare_op=ALU.not_equal, fill=1.0,
                                    base=0, pattern=[[-1, P]], channel_multiplier=1)
            nc.gpsimd.affine_select(out=earlier[:, :, :], in_=earlier[:, :, :], compare_op=ALU.is_gt,
                                    fill=0.0, base=0, pattern=[[1, EXPERTS], [-1, EXPERTS]],
                                    channel_multiplier=0).then_inc(pool_ready, 1)

            def body(i, parity, active):
                for z, kind, n in STEPS:
                    if z not in active:
                        continue
                    if kind == "norm":
                        pool.wait_ge(norm_steps[z].sem, norm_steps[z].at(i))
                        nc.gpsimd.tensor_tensor(rstd[z][:, :], variance[z][:, :], minus_half[:, :],
                                                ALU.pow).then_inc(rstd_done[z].sem, 1)
                        if z == CROSS_IN:
                            if residual_added[SELF_OUT].begun(i - 1):
                                pool.wait_ge(residual_added[SELF_OUT].sem, residual_added[SELF_OUT].at(i - 1))
                            if residual_added[CROSS_OUT].begun(i - 1):
                                pool.wait_ge(residual_added[CROSS_OUT].sem, residual_added[CROSS_OUT].at(i - 1))
                            h = slot_of(parity, z)
                            nc.gpsimd.tensor_tensor(
                                x1_b4[h][:, :, :], x1[h][:, :, :],
                                b4_sb[:, :].unsqueeze(1).to_broadcast([P, NSEQ, D]),
                                ALU.add).then_inc(x1_b4_done.sem, 1)
                    if kind == "latent":
                        pool.wait_ge(latent_steps.sem, latent_steps.at(i))
                        nc.gpsimd.tensor_tensor(lat_rstd[:, :], lat_variance[:, :], minus_half[:, :],
                                                ALU.pow).then_inc(latent_rstd.sem, 1)
                    if kind == "rotary":
                        pool.wait_ge(rotary_multiplied.sem, rotary_multiplied.at(i, n + 1))
                        if rotary_lo_done.begun(i, n):
                            pool.wait_ge(rotary_lo_done.sem, rotary_lo_done.at(i, n))
                        nc.gpsimd.tensor_tensor(rotary_sum[:, :], rotary_parts[:, 0, :], rotary_parts[:, 1, :],
                                                ALU.add).then_inc(rotary_added.sem, 1)
                        pool.wait_ge(rotary_hi_done.sem, rotary_hi_done.at(i, n + 1))
                        if n == 0:
                            if qk_stored[SELF_OUT].begun(i - 1):
                                pool.wait_ge(qk_stored[SELF_OUT].sem, qk_stored[SELF_OUT].at(i - 1))
                        nc.gpsimd.tensor_tensor(self_qk_lo[:, n, :], rotary_sum[:, :], self_qk_hi[:, n, :],
                                                ALU.subtract).then_inc(rotary_lo_done.sem, 1)
                    if kind == "split":
                        pool.wait_ge(hidden_hi_done.sem, hidden_hi_done.at(i, n + 1))
                        nc.gpsimd.tensor_tensor(hidden_lo[:, n % 2, :], hidden_c[:, n % 2, :], hidden_hi[:, n % 2, :],
                                                ALU.subtract).then_inc(hidden_lo_done.sem, 1)

            run(pool, body)

        @block.scalar
        def _(act):
            act.wait_ge(pool_ready, 1)
            nc.scalar.copy(ident16[:, :], ident[:, :])
            nc.scalar.copy(ident_bf[:, :], ident[:, :])
            nc.scalar.mul(minus_ident[:, :], ident[:, :], -1.0)
            act.wait_ge(constants_loaded, 16 * 10)
            nc.scalar.mul(gamma_scaled[:, :], gamma_sb[:, :], 1.0 / WS)
            nc.scalar.mul(b1_scaled[:, :], b1_sb[:, :], WS)
            nc.scalar.mul(b2_scaled[:, :], b2_sb[:, :], WS)
            for g in range(HG):
                last = nc.scalar.copy(causal_sb[:, :, g * SEQ:(g + 1) * SEQ], causal_f32[:, :, :])
            last.then_inc(act_ready, 1)
            for n, (src, hi, _) in enumerate(chunks):
                act.wait_ge(chunk_loaded[n % 2], 16 * (n // 2 + 1))
                nc.scalar.mul(hi, staging[n % 2][:, 0:src.shape[1]], WS).then_inc(chunk_hi, 1)
            act.wait_ge(act_ready, 1)
            act.wait_ge(chunk_lo, len(chunks))

            def body(i, parity, active):
                for z, kind, n in STEPS:
                    if z not in active:
                        continue
                    if kind == "norm_turn":
                        act.wait_ge(norm_turned[z].sem, norm_turned[z].at(i))
                        src = coef_bank if z == FFN else setup_bank
                        nc.scalar.copy(xT_hi[z][:, :, :].rearrange("p k t -> p (k t)"),
                                       src[:, :]).then_inc(xT_hi_done[z].sem, 1)
                    if kind == "rotary":
                        act.wait_ge(rotary_added.sem, rotary_added.at(i, n + 1))
                        if n == 0:
                            if qk_stored[SELF_OUT].begun(i - 1):
                                act.wait_ge(qk_stored[SELF_OUT].sem, qk_stored[SELF_OUT].at(i - 1))
                        nc.scalar.copy(self_qk_hi[:, n, :], rotary_sum[:, :]).then_inc(rotary_hi_done.sem, 1)
                    if kind == "latent_turn":
                        act.wait_ge(latent_turned.sem, latent_turned.at(i))
                        if latent_split.begun(i - 1):
                            act.wait_ge(latent_split.sem, latent_split.at(i - 1))
                        nc.scalar.activation(latT[:, :], setup_bank[:, 0:T], ACT.Identity, bias=beta_sb[:, 0:1],
                                             scale=gamma_scaled[:, 0:1]).then_inc(latent_affine.sem, 1)
                        act.wait_ge(latent_affine.sem, latent_affine.at(i))
                        nc.scalar.copy(latT_split[:, :], latT[:, :]).then_inc(latent_hi_done.sem, 1)
                    if kind == "latent_values":
                        act.wait_ge(values_projected[SELF_OUT].sem, values_projected[SELF_OUT].at(i))
                        h = slot_of(parity, SELF_IN)
                        nc.scalar.mul(values[SELF_OUT][h][:, :, :, 0:HD],
                                      setup_bank[:, :].rearrange("p (s h d) -> p s h d", s=NSEQ, h=HEADS),
                                      1.0 / WS).then_inc(values_ready[SELF_OUT].sem, 1)
                    if kind == "context_turn":
                        act.wait_ge(ctx_turned.sem, ctx_turned.at(i))
                        nc.scalar.copy(ctxT_hi[:, :, :].rearrange("p k t -> p (k t)"),
                                       setup_bank[:, :]).then_inc(ctx_hi_done.sem, 1)
                    if kind in ("keys", "queries"):
                        m0, bias, k = (2, b2_scaled, 1) if kind == "keys" else (0, b1_scaled, 2)
                        act.wait_ge(qk_projected.sem, qk_projected.at(i, k))
                        if kind == "keys":
                            if qk_stored[CROSS_OUT].begun(i - 1):
                                act.wait_ge(qk_stored[CROSS_OUT].sem, qk_stored[CROSS_OUT].at(i - 1))
                        for m in range(KT):
                            last = nc.scalar.activation(cross_qk_hi[:, m0 + m, :], setup_bank[:, m * T:(m + 1) * T],
                                                        ACT.Identity, bias=bias[:, m:m + 1])
                        last.then_inc(qk_hi_done.sem, 1)
                    if kind == "weights":
                        act.wait_ge(weighed[z].sem, weighed[z].at(i, n + 1))
                        g = n % GROUPS
                        nc.scalar.activation(probs[z][:, g * HG:(g + 1) * HG, :],
                                             score_bank[z][:, :].rearrange("p (h q) -> p h q", h=HG), ACT.Exp,
                                             scale=SCORE_SCALE).then_inc(exped[z].sem, 1)
                    if kind == "turn":
                        act.wait_ge(valued[z].sem, valued[z].at(i, (n + 1) * GROUPS))
                        nc.scalar.copy(outT[z][:, :], out_bank[z][:, :]).then_inc(out_copied[z].sem, 1)
                    if kind == "feature_turn":
                        act.wait_ge(heads_turned[z].sem, heads_turned[z].at(i))
                        nc.scalar.copy(headsT_hi[z][:, :, :].rearrange("p k t -> p (k t)"),
                                       out_bank[z][:, :]).then_inc(heads_hi_done[z].sem, 1)
                    if kind == "choose":
                        act.wait_ge(choose_steps.sem, choose_steps.at(i, 3))
                        nc.scalar.activation(exps[:, :, :], shifted[:, :, :], ACT.Exp).then_inc(router_exped.sem, 1)
                    if kind == "hidden":
                        act.wait_ge(gate_up_done.sem, gate_up_done.at(i, n + 1))
                        nc.scalar.activation(tanh_sb[:, n % 2, :], gate_up_bank[:, 0:T], ACT.Tanh,
                                             scale=0.5 / WS).then_inc(tanh_done.sem, 1)
                    if kind == "split":
                        act.wait_ge(hidden_done.sem, hidden_done.at(i, n + 1))
                        if n >= SHARED_TILES:
                            act.wait_ge(hidden_scaled.sem, hidden_scaled.at(i, n - SHARED_TILES + 1))
                        nc.scalar.copy(hidden_hi[:, n % 2, :], hidden_c[:, n % 2, :]).then_inc(hidden_hi_done.sem, 1)

            run(act, body)

        @block.vector
        def _(dve):
            for n, (src, hi, lo) in enumerate(chunks):
                dve.wait_ge(chunk_hi, n + 1)
                nc.vector.scalar_tensor_tensor(out=lo, in0=staging[n % 2][:, 0:src.shape[1]], scalar=WS, in1=hi,
                                               op0=ALU.mult, op1=ALU.subtract).then_inc(chunk_lo, 1)
            dve.wait_ge(act_ready, 1)
            dve.wait_ge(pool_ready, 1)

            def normalise(i, parity, z):
                src = {SELF_IN: x_in, CROSS_IN: x1[slot_of(parity, CROSS_IN)], FFN: x2[slot_of(parity, FFN)]}[z]
                if z == SELF_IN:
                    dve.wait_ge(x_loaded.sem, x_loaded.at(i))
                if z == CROSS_IN:
                    if residual_added[SELF_OUT].begun(i - 1):
                        dve.wait_ge(residual_added[SELF_OUT].sem, residual_added[SELF_OUT].at(i - 1))
                if z == FFN:
                    if residual_added[CROSS_OUT].begun(i - 1):
                        dve.wait_ge(residual_added[CROSS_OUT].sem, residual_added[CROSS_OUT].at(i - 1))
                for s in range(NSEQ):
                    last = nc.vector.bn_stats(stats[z][:, s, :], src[:, s, :])
                last.then_inc(norm_steps[z].sem, 1)
                dve.wait_ge(norm_steps[z].sem, norm_steps[z].at(i, 1))
                nc.vector.memset(wait_holder[:, :], 0.0)
                for s in range(NSEQ):
                    last = nc.vector.bn_aggr(moments[z][:, s, :], stats[z][:, s, :])
                last.then_inc(norm_steps[z].sem, 1)
                dve.wait_ge(norm_steps[z].sem, norm_steps[z].at(i, 2))
                nc.vector.tensor_scalar(variance[z][:, :], moments[z][:, :, 1], EPS, None,
                                        ALU.add).then_inc(norm_steps[z].sem, 1)
                dve.wait_ge(rstd_done[z].sem, rstd_done[z].at(i))
                for s in range(NSEQ):
                    last = nc.vector.tensor_scalar(normed[z][:, s, :], src[:, s, :], moments[z][:, s, 0:1],
                                                   rstd[z][:, s:s + 1], ALU.subtract, ALU.mult)
                last.then_inc(norm_done[z].sem, 1)

            def remainder(lo, src, hi):
                return nc.vector.tensor_tensor(lo[:, :, :].rearrange("p k t -> p (k t)"), src[:, :],
                                               hi[:, :, :].rearrange("p k t -> p (k t)"), ALU.subtract)

            def choose(i):
                def step(n, instruction):
                    instruction.then_inc(choose_steps.sem, 1)
                    if choose_steps.begun(i, n):
                        dve.wait_ge(choose_steps.sem, choose_steps.at(i, n))
                v = nc.vector
                pair = [P, NSEQ, EXPERTS]
                quad = [P, EXPERTS, EXPERTS]
                dve.wait_ge(routed.sem, routed.at(i))
                step(1, v.tensor_scalar(logits[:, :, :], coef_bank[:, 0:NSEQ * EXPERTS].rearrange(
                    "p (s e) -> p s e", s=NSEQ), 1.0 / WS, None, ALU.mult))
                step(2, v.reduce_max(top_logit[:, :], logits[:, :, :], AX_X))
                step(3, v.tensor_tensor(shifted[:, :, :], logits[:, :, :],
                                        top_logit[:, :].unsqueeze(2).to_broadcast(pair), ALU.subtract))
                for s in range(NSEQ):
                    mine = logits[:, s, :].unsqueeze(2).to_broadcast(quad)
                    other = logits[:, s, :].unsqueeze(1).to_broadcast(quad)
                    v.tensor_tensor(greater[:, s, :, :], other, mine, ALU.is_gt)
                    last = v.tensor_tensor(equal[:, s, :, :], other, mine, ALU.is_equal)
                step(4, last)
                for s in range(NSEQ):
                    last = v.tensor_tensor(equal[:, s, :, :], equal[:, s, :, :], earlier[:, :, :], ALU.mult)
                step(5, last)
                step(6, v.tensor_tensor(greater[:, :, :, :], greater[:, :, :, :], equal[:, :, :, :], ALU.add))
                step(7, v.reduce_sum(rank[:, :, :], greater[:, :, :, :], AX_X))
                dve.wait_ge(router_exped.sem, router_exped.at(i))
                step(8, v.reduce_sum(exp_sum[:, :], exps[:, :, :], AX_X))
                step(9, v.reciprocal(exp_inv[:, :], exp_sum[:, :]))
                step(10, v.tensor_tensor(router_probs[:, :, :], exps[:, :, :],
                                         exp_inv[:, :].unsqueeze(2).to_broadcast(pair), ALU.mult))
                step(11, v.scalar_tensor_tensor(out=coef[:, :, :], in0=rank[:, :, :], scalar=TOP_K - 0.5,
                                                in1=router_probs[:, :, :], op0=ALU.is_lt, op1=ALU.mult))
                step(12, v.tensor_copy(coef_hi[:, :, :], coef[:, :, :]))
                step(13, v.tensor_tensor(coef_lo[:, :, :], coef[:, :, :], coef_hi[:, :, :], ALU.subtract))

            def body(i, parity, active):
                for z, kind, n in STEPS:
                    if z not in active:
                        continue
                    if kind == "norm":
                        normalise(i, parity, z)
                    if kind == "norm_turn":
                        dve.wait_ge(xT_hi_done[z].sem, xT_hi_done[z].at(i))
                        remainder(xT_lo[z], coef_bank if z == FFN else setup_bank,
                                  xT_hi[z]).then_inc(xT_lo_done[z].sem, 1)
                    if kind == "rotary":
                        dve.wait_ge(rotary_projected.sem, rotary_projected.at(i, n + 1))
                        if rotary_added.begun(i, n):
                            dve.wait_ge(rotary_added.sem, rotary_added.at(i, n))
                        nc.vector.tensor_tensor(rotary_parts[:, :, :].rearrange("p a t -> p (a t)"), setup_bank[:, :],
                                                rotary_sb[:, :, :].rearrange("p a t -> p (a t)"),
                                                ALU.mult).then_inc(rotary_multiplied.sem, 1)
                    if kind == "latent":
                        dve.wait_ge(latent_projected.sem, latent_projected.at(i))
                        for s in range(NSEQ):
                            last = nc.vector.bn_stats(lat_stats[:, s, :], setup_bank[:, s * LATENT:(s + 1) * LATENT])
                        last.then_inc(latent_steps.sem, 1)
                        dve.wait_ge(latent_steps.sem, latent_steps.at(i, 1))
                        nc.vector.memset(wait_holder[:, :], 0.0)
                        for s in range(NSEQ):
                            last = nc.vector.bn_aggr(lat_moments[:, s, :], lat_stats[:, s, :])
                        last.then_inc(latent_steps.sem, 1)
                        dve.wait_ge(latent_steps.sem, latent_steps.at(i, 2))
                        nc.vector.tensor_scalar(lat_variance[:, :], lat_moments[:, :, 1], 1.0 / (WS * WS), EPS,
                                                ALU.mult, ALU.add).then_inc(latent_steps.sem, 1)
                        dve.wait_ge(latent_rstd.sem, latent_rstd.at(i))
                        for s in range(NSEQ):
                            for k in range(2):
                                last = nc.vector.tensor_scalar(
                                    lat_twice[:, s, k, :], setup_bank[:, s * LATENT:(s + 1) * LATENT],
                                    lat_moments[:, s, 0:1], lat_rstd[:, s:s + 1], ALU.subtract, ALU.mult)
                        last.then_inc(latent_normed.sem, 1)
                    if kind == "latent_turn":
                        dve.wait_ge(latent_hi_done.sem, latent_hi_done.at(i))
                        nc.vector.tensor_tensor(latT_split[LATENT:P, :], latT[LATENT:P, :],
                                                latT_split[LATENT:P, :], ALU.subtract).then_inc(latent_split.sem, 1)
                    if kind == "context_turn":
                        dve.wait_ge(ctx_hi_done.sem, ctx_hi_done.at(i))
                        remainder(ctxT_lo, setup_bank, ctxT_hi).then_inc(ctx_lo_done.sem, 1)
                    if kind in ("keys", "queries"):
                        m0, bias, k = (2, b2_scaled, 1) if kind == "keys" else (0, b1_scaled, 2)
                        dve.wait_ge(qk_hi_done.sem, qk_hi_done.at(i, k))
                        if kind == "keys":
                            if qk_stored[CROSS_OUT].begun(i - 1):
                                dve.wait_ge(qk_stored[CROSS_OUT].sem, qk_stored[CROSS_OUT].at(i - 1))
                        for m in range(KT):
                            last = nc.vector.scalar_tensor_tensor(
                                out=cross_qk_lo[:, m0 + m, :], in0=setup_bank[:, m * T:(m + 1) * T],
                                scalar=bias[:, m:m + 1], in1=cross_qk_hi[:, m0 + m, :],
                                op0=ALU.add, op1=ALU.subtract)
                        last.then_inc(qk_lo_done.sem, 1)
                    if kind == "context_values":
                        dve.wait_ge(values_projected[CROSS_OUT].sem, values_projected[CROSS_OUT].at(i))
                        h = slot_of(parity, CROSS_IN)
                        for s in range(NSEQ):
                            last = nc.vector.scalar_tensor_tensor(
                                out=values[CROSS_OUT][h][:, s, :, 0:HD],
                                in0=setup_bank[:, s * D:(s + 1) * D].rearrange("p (h d) -> p h d", h=HEADS),
                                scalar=1.0 / WS, in1=b3_sb[:, :].rearrange("p (h d) -> p h d", h=HEADS),
                                op0=ALU.mult, op1=ALU.add)
                        last.then_inc(values_ready[CROSS_OUT].sem, 1)
                    if kind == "scores":
                        dve.wait_ge(scored[z].sem, scored[z].at(i, n + 1))
                        s, g = divmod(n, GROUPS)
                        nc.vector.reduce_max(top_score[z][:, s, g * HG:(g + 1) * HG],
                                             score_bank[z][:, :].rearrange("p (h k) -> p h k", h=HG),
                                             AX_X).then_inc(maxed[z].sem, 1)
                    if kind == "turn":
                        dve.wait_ge(out_turned[z].sem, out_turned[z].at(i, n + 1))
                        summed = out_bank[z][:, :].rearrange("p (g h w) -> p g h w", g=GROUPS, w=VW)
                        inv = inverse[z][:, :].rearrange("p (g h) -> p g h", g=GROUPS)
                        nc.vector.reciprocal(inv, summed[:, :, :, HD]).then_inc(inverted[z].sem, 1)
                        dve.wait_ge(inverted[z].sem, inverted[z].at(i, n + 1))
                        heads = heads_out[z][:, n, :].rearrange("p (h d) -> p h d", d=HD)
                        nc.vector.tensor_tensor(
                            heads, out_bank[z][:, :].rearrange("p (h w) -> p h w", w=VW)[:, :, 0:HD],
                            inverse[z][:, :].unsqueeze(2).to_broadcast([P, HEADS, HD]),
                            ALU.mult).then_inc(divided[z].sem, 1)
                    if kind == "feature_turn":
                        dve.wait_ge(heads_hi_done[z].sem, heads_hi_done[z].at(i))
                        remainder(headsT_lo[z], out_bank[z], headsT_hi[z]).then_inc(heads_lo_done[z].sem, 1)
                    if kind == "project":
                        dve.wait_ge(projected[z].sem, projected[z].at(i))
                        h = slot_of(parity, z)
                        if z == SELF_OUT:
                            dve.wait_ge(x_again_loaded.sem, x_again_loaded.at(i))
                            if x1_b4_done.begun(i - 1):
                                dve.wait_ge(x1_b4_done.sem, x1_b4_done.at(i - 1))
                            dst, src = x1[h], x_again
                        else:
                            if x1_b4_done.begun(i - 1):
                                dve.wait_ge(x1_b4_done.sem, x1_b4_done.at(i - 1))
                            if result_done.begun(i - 1):
                                dve.wait_ge(result_done.sem, result_done.at(i - 1))
                            dst, src = x2[h], x1_b4[h]
                        nc.vector.scalar_tensor_tensor(
                            out=dst[:, :, :].rearrange("p s d -> p (s d)"), in0=out_bank[z][:, :], scalar=1.0 / WS,
                            in1=src[:, :, :].rearrange("p s d -> p (s d)"), op0=ALU.mult,
                            op1=ALU.add).then_inc(residual_added[z].sem, 1)
                    if kind == "choose":
                        choose(i)
                    if kind == "hidden":
                        dve.wait_ge(tanh_done.sem, tanh_done.at(i, n + 1))
                        if hidden_done.begun(i, n):
                            dve.wait_ge(hidden_done.sem, hidden_done.at(i, n))
                        nc.vector.scalar_tensor_tensor(out=gated[:, :], in0=tanh_sb[:, n % 2, :], scalar=1.0,
                                                       in1=gate_up_bank[:, 0:T], op0=ALU.add,
                                                       op1=ALU.mult).then_inc(gated_done.sem, 1)
                        dve.wait_ge(gated_done.sem, gated_done.at(i, n + 1))
                        if hidden_lo_done.begun(i, n - 1):
                            dve.wait_ge(hidden_lo_done.sem, hidden_lo_done.at(i, n - 1))
                        if n > SHARED_TILES:
                            if hidden_scaled.begun(i, n - SHARED_TILES):
                                dve.wait_ge(hidden_scaled.sem, hidden_scaled.at(i, n - SHARED_TILES))
                        dst = hidden_c[:, n % 2, :] if n < SHARED_TILES else hidden[:, :]
                        nc.vector.scalar_tensor_tensor(out=dst, in0=gate_up_bank[:, T:2 * T], scalar=0.5 / WS,
                                                       in1=gated[:, :], op0=ALU.mult,
                                                       op1=ALU.mult).then_inc(hidden_done.sem, 1)
                        if n >= SHARED_TILES:
                            e = n - SHARED_TILES
                            dve.wait_ge(hidden_done.sem, hidden_done.at(i, n + 1))
                            dve.wait_ge(coef_spread.sem, coef_spread.at(i, e + 1))
                            nc.vector.tensor_tensor(hidden_c[:, n % 2, :], hidden[:, :], coef_bank[:, 0:T],
                                                    ALU.mult).then_inc(hidden_scaled.sem, 1)
                    if kind == "finish":
                        dve.wait_ge(down_done.sem, down_done.at(i))
                        if result_stored.begun(i - 1):
                            dve.wait_ge(result_stored.sem, result_stored.at(i - 1))
                        nc.vector.scalar_tensor_tensor(
                            out=result[:, :, :].rearrange("p s d -> p (s d)"), in0=down_bank[:, :],
                            scalar=1.0 / (WS * WS), in1=x2[slot_of(parity, FFN)][:, :, :].rearrange("p s d -> p (s d)"),
                            op0=ALU.mult, op1=ALU.add).then_inc(result_done.sem, 1)

            run(dve, body)

        @block.tensor
        def _(pe):
            mm = nc.tensor.matmul
            pe.wait_ge(chunk_lo, len(chunks))
            pe.wait_ge(act_ready, 1)
            pe.wait_ge(pool_ready, 1)

            def split_product(dst, pairs, opened=False, closes=True):
                n = 0
                for (lh, ll), (rh, rl) in pairs:
                    for a, b in ((lh, rh), (lh, rl), (ll, rh)):
                        n += 1
                        last = mm(dst, a, b, start=(n == 1 and not opened),
                                  stop=(closes and n == 3 * len(pairs)), skip_group_check=True)
                return last

            def turn(dst_bank, src):
                for kt in range(KT):
                    for s in range(NSEQ):
                        c = (kt * NSEQ + s) * SEQ
                        last = nc.tensor.transpose(dst_bank[:, c:c + SEQ], src[:, s, kt * P:(kt + 1) * P], ident[:, :])
                return last

            def setup_free(i, active, z, first):
                if not first:
                    return
                if z == SELF_IN:
                    if values_ready[SELF_OUT].begun(i - 1):
                        pe.wait_ge(values_ready[SELF_OUT].sem, values_ready[SELF_OUT].at(i - 1))
                    if not isinstance(i, int) or i - 1 >= CROSS_IN:
                        if values_ready[CROSS_OUT].begun(i - 1):
                            pe.wait_ge(values_ready[CROSS_OUT].sem, values_ready[CROSS_OUT].at(i - 1))
                else:
                    if values_ready[CROSS_OUT].begun(i - 1):
                        pe.wait_ge(values_ready[CROSS_OUT].sem, values_ready[CROSS_OUT].at(i - 1))
                    if SELF_IN in active:
                        pe.wait_ge(values_ready[SELF_OUT].sem, values_ready[SELF_OUT].at(i))

            def tokens(hi, lo, kt, s):
                a = slice(s * SEQ, (s + 1) * SEQ)
                return hi[:, kt, a], lo[:, kt, a]

            def body(i, parity, active):
                for z, kind, n in STEPS:
                    if z not in active:
                        continue
                    if kind == "norm_turn":
                        pe.wait_ge(norm_done[z].sem, norm_done[z].at(i))
                        if z == FFN:
                            if hidden_scaled.begun(i - 1):
                                pe.wait_ge(hidden_scaled.sem, hidden_scaled.at(i - 1))
                            turn(coef_bank, normed[z]).then_inc(norm_turned[z].sem, 1)
                        else:
                            if z == SELF_IN:
                                setup_free(i, active, z, True)
                            else:
                                pe.wait_ge(ctx_lo_done.sem, ctx_lo_done.at(i))
                            turn(setup_bank, normed[z]).then_inc(norm_turned[z].sem, 1)
                    if kind == "rotary":
                        if n == 0:
                            pe.wait_ge(xT_lo_done[SELF_IN].sem, xT_lo_done[SELF_IN].at(i))
                        if n == 1:
                            pe.wait_ge(latent_normed.sem, latent_normed.at(i))
                        if n == 2:
                            pe.wait_ge(latent_split.sem, latent_split.at(i))
                        if n == 3:
                            pe.wait_ge(rotary_multiplied.sem, rotary_multiplied.at(i, 3))
                        for turned in range(2):
                            dst = setup_bank[:, turned * T:(turned + 1) * T]
                            if n < 2:
                                name = ("q", "q_turned")[turned]
                                last = split_product(dst, [(w(name, kt, n * P, P), (xT_hi[SELF_IN][:, kt, :],
                                                                                   xT_lo[SELF_IN][:, kt, :]))
                                                           for kt in range(KT)])
                            else:
                                a = LAT[("k", "k_turned")[turned]] + (n - 2) * P
                                mm(dst, lat_hi[:, a:a + P], latT_split[:, :], start=True, stop=False)
                                last = mm(dst, lat_lo[:, a:a + P], latT_split[:, :], start=False, stop=True)
                        last.then_inc(rotary_projected.sem, 1)
                    if kind == "latent":
                        pe.wait_ge(rotary_multiplied.sem, rotary_multiplied.at(i, 1))
                        for s in range(NSEQ):
                            last = split_product(setup_bank[:, s * LATENT:(s + 1) * LATENT],
                                                 [(tokens(xT_hi[SELF_IN], xT_lo[SELF_IN], kt, s),
                                                   w("down_latent", kt, 0, LATENT)) for kt in range(KT)])
                        last.then_inc(latent_projected.sem, 1)
                    if kind == "latent_turn":
                        pe.wait_ge(latent_normed.sem, latent_normed.at(i))
                        pe.wait_ge(rotary_multiplied.sem, rotary_multiplied.at(i, 2))
                        for s in range(NSEQ):
                            last = nc.tensor.transpose(setup_bank[:, s * SEQ:(s + 1) * SEQ],
                                                       lat_twice[:, s, :, :].rearrange("p a l -> p (a l)"), ident[:, :])
                        last.then_inc(latent_turned.sem, 1)
                    if kind == "latent_values":
                        pe.wait_ge(rotary_multiplied.sem, rotary_multiplied.at(i, 4))
                        for s in range(NSEQ):
                            dst = setup_bank[:, s * D:(s + 1) * D]
                            lat = latT_split[:, s * SEQ:(s + 1) * SEQ]
                            mm(dst, lat, lat_hi[:, LAT["v"]:LAT["v"] + D], start=True, stop=False)
                            last = mm(dst, lat, lat_lo[:, LAT["v"]:LAT["v"] + D], start=False, stop=True)
                        last.then_inc(values_projected[SELF_OUT].sem, 1)
                    if kind == "context_turn":
                        pe.wait_ge(ctx_loaded.sem, ctx_loaded.at(i))
                        setup_free(i, active, z, True)
                        turn(setup_bank, ctx_in).then_inc(ctx_turned.sem, 1)
                    if kind in ("keys", "queries"):
                        if kind == "keys":
                            pe.wait_ge(xT_lo_done[CROSS_IN].sem, xT_lo_done[CROSS_IN].at(i))
                            name, hi, lo = "cross_k", ctxT_hi, ctxT_lo
                        else:
                            pe.wait_ge(qk_lo_done.sem, qk_lo_done.at(i, 1))
                            name, hi, lo = "cross_q", xT_hi[CROSS_IN], xT_lo[CROSS_IN]
                        for m in range(KT):
                            last = split_product(setup_bank[:, m * T:(m + 1) * T],
                                                 [(w(name, kt, m * P, P), (hi[:, kt, :], lo[:, kt, :]))
                                                  for kt in range(KT)])
                        last.then_inc(qk_projected.sem, 1)
                    if kind == "context_values":
                        pe.wait_ge(qk_lo_done.sem, qk_lo_done.at(i, 2))
                        for s in range(NSEQ):
                            last = split_product(setup_bank[:, s * D:(s + 1) * D],
                                                 [(tokens(ctxT_hi, ctxT_lo, kt, s), w("cross_v", kt, 0, D))
                                                  for kt in range(KT)])
                        last.then_inc(values_projected[CROSS_OUT].sem, 1)
                    if kind in ("scores", "weights"):
                        s, g = divmod(n, GROUPS)
                        h = slot_of(parity, z)
                        a = slice(s * SEQ, (s + 1) * SEQ)
                        if kind == "scores":
                            if n == 0:
                                if qk_packed[z].begun(i - 1):
                                    pe.wait_ge(qk_packed[z].sem, qk_packed[z].at(i - 1))
                            if g == 0:
                                if exped[z].begun(i, s * GROUPS):
                                    pe.wait_ge(exped[z].sem, exped[z].at(i, s * GROUPS))
                            else:
                                if maxed[z].begun(i, n):
                                    pe.wait_ge(maxed[z].sem, maxed[z].at(i, n))
                        else:
                            if g == 0:
                                pe.wait_ge(maxed[z].sem, maxed[z].at(i, (s + 1) * GROUPS))
                            else:
                                if exped[z].begun(i, n):
                                    pe.wait_ge(exped[z].sem, exped[z].at(i, n))
                        causal_mask = z == SELF_OUT
                        if causal_mask:
                            mm(score_bank[z][:, :], ident_bf[:, :], causal_sb[:, int(kind == "weights"), :],
                               start=True, stop=False, skip_group_check=True)
                        for k in range(HG):
                            head = g * HG + k
                            dst = score_bank[z][:, k * SEQ:(k + 1) * SEQ]
                            q = q_packed[z][h][:, head, a]
                            keys = k_packed[z][h][:, head // 2, a]
                            if kind == "scores":
                                last = mm(dst, q, keys, start=not causal_mask, stop=True, skip_group_check=True)
                            else:
                                mm(dst, keys, q, start=not causal_mask, stop=False, skip_group_check=True)
                                top = top_score[z][:, s, head:head + 1].to_broadcast([P, P])
                                last = mm(dst, top, minus_ident[:, :], start=False, stop=True, skip_group_check=True)
                        last.then_inc((scored if kind == "scores" else weighed)[z].sem, 1)
                    if kind == "values":
                        s, g = divmod(n, GROUPS)
                        pe.wait_ge(exped[z].sem, exped[z].at(i, n + 1))
                        if n == 0:
                            if values_ready[z].begun(i - 1):
                                pe.wait_ge(values_ready[z].sem, values_ready[z].at(i - 1))
                            if residual_added[z].begun(i - 1):
                                pe.wait_ge(residual_added[z].sem, residual_added[z].at(i - 1))
                        if n == GROUPS:
                            pe.wait_ge(divided[z].sem, divided[z].at(i, 1))
                        for k in range(HG):
                            head = g * HG + k
                            last = mm(out_bank[z][VW * k:VW * (k + 1), g * SEQ:(g + 1) * SEQ],
                                      values[z][slot_of(parity, z)][:, s, head, :], probs[z][:, head, :],
                                      start=True, stop=True, tile_position=(0, VW * k), skip_group_check=True)
                        last.then_inc(valued[z].sem, 1)
                    if kind == "turn":
                        pe.wait_ge(out_copied[z].sem, out_copied[z].at(i, n + 1))
                        for g in range(GROUPS):
                            last = nc.tensor.transpose(out_bank[z][:, g * SEQ:(g + 1) * SEQ],
                                                       outT[z][:, g * SEQ:(g + 1) * SEQ], ident[:, :])
                        last.then_inc(out_turned[z].sem, 1)
                    if kind == "feature_turn":
                        pe.wait_ge(divided[z].sem, divided[z].at(i))
                        turn(out_bank[z], heads_out[z]).then_inc(heads_turned[z].sem, 1)
                    if kind == "project":
                        pe.wait_ge(heads_lo_done[z].sem, heads_lo_done[z].at(i))
                        name = "self_out" if z == SELF_OUT else "cross_out"
                        for s in range(NSEQ):
                            last = split_product(out_bank[z][:, s * D:(s + 1) * D],
                                                 [(tokens(headsT_hi[z], headsT_lo[z], kt, s), w(name, kt, 0, D))
                                                  for kt in range(KT)])
                        last.then_inc(projected[z].sem, 1)
                    if kind == "router":
                        pe.wait_ge(xT_lo_done[FFN].sem, xT_lo_done[FFN].at(i))
                        for s in range(NSEQ):
                            last = split_product(coef_bank[:, s * EXPERTS:(s + 1) * EXPERTS],
                                                 [(tokens(xT_hi[FFN], xT_lo[FFN], kt, s), w("router", kt, 0, EXPERTS))
                                                  for kt in range(KT)])
                        last.then_inc(routed.sem, 1)
                    if kind == "hidden":
                        if n == 0:
                            pe.wait_ge(xT_lo_done[FFN].sem, xT_lo_done[FFN].at(i))
                            if hidden_done.begun(i - 1):
                                pe.wait_ge(hidden_done.sem, hidden_done.at(i - 1))
                        else:
                            if hidden_done.begun(i, n):
                                pe.wait_ge(hidden_done.sem, hidden_done.at(i, n))
                        for half, names in enumerate((("shared_gate", "gate"), ("shared_up", "up"))):
                            name, c = (names[0], n * P) if n < SHARED_TILES else (names[1], (n - SHARED_TILES) * P)
                            last = split_product(gate_up_bank[:, half * T:(half + 1) * T],
                                                 [(w(name, kt, c, P), (xT_hi[FFN][:, kt, :], xT_lo[FFN][:, kt, :]))
                                                  for kt in range(KT)])
                        last.then_inc(gate_up_done.sem, 1)
                        if n >= SHARED_TILES:
                            e = n - SHARED_TILES
                            if e == 0:
                                pe.wait_ge(choose_steps.sem, choose_steps.at(i))
                            else:
                                if hidden_scaled.begun(i, e):
                                    pe.wait_ge(hidden_scaled.sem, hidden_scaled.at(i, e))
                            for s in range(NSEQ):
                                dst = coef_bank[:, s * SEQ:(s + 1) * SEQ]
                                mm(dst, coef_hi[:, s, e:e + 1].to_broadcast([P, P]), ident16[:, :],
                                   start=True, stop=False)
                                last = mm(dst, coef_lo[:, s, e:e + 1].to_broadcast([P, P]), ident16[:, :],
                                          start=False, stop=True)
                            last.then_inc(coef_spread.sem, 1)
                    if kind == "down":
                        if n == 0:
                            if result_done.begun(i - 1):
                                pe.wait_ge(result_done.sem, result_done.at(i - 1))
                        pe.wait_ge(hidden_lo_done.sem, hidden_lo_done.at(i, n + 1))
                        if n < SHARED_TILES:
                            weights = w("shared_down", n, 0, D)
                        else:
                            c = (n - SHARED_TILES) * D
                            weights = down_hi[:, c:c + D], down_lo[:, c:c + D]
                        for s in range(NSEQ):
                            a = slice(s * SEQ, (s + 1) * SEQ)
                            last = split_product(down_bank[:, s * D:(s + 1) * D],
                                                 [((hidden_hi[:, n % 2, a], hidden_lo[:, n % 2, a]), weights)],
                                                 opened=not (n == 0 and s == 0), closes=n == TILES - 1)
                        last.then_inc(down_done.sem, 1)

            run(pe, body)


def _layout(a):
    f = np.float32
    turned = np.arange(D).reshape(HEADS, 2, HD // 2)[:, ::-1].reshape(-1)
    wide = np.concatenate([
        a["L0_attn_W_q"], a["L0_attn_W_q"][:, turned], a["L0_attn_W_dkv"], a["L0_attn_W_o"],
        a["L0_xattn_w1"].T, a["L0_xattn_w2"].T, a["L0_xattn_w3"].T, a["L0_xattn_w4"].T,
        a["L0_ffn_shared_gate"], a["L0_ffn_shared_up"], a["L0_ffn_shared_down"], a["L0_ffn_router"],
        a["L0_ffn_experts_gate"].transpose(1, 0, 2).reshape(D, EXPERTS * P),
        a["L0_ffn_experts_up"].transpose(1, 0, 2).reshape(D, EXPERTS * P)], axis=1)
    expert_down = a["L0_ffn_experts_down"].transpose(1, 0, 2).reshape(P, EXPERTS * D)
    lat = np.concatenate([a["L0_attn_W_uk"], a["L0_attn_W_uk"][:, turned], a["L0_attn_W_uv"]], axis=1)
    lat = np.concatenate([lat, lat], axis=0)
    twice = lambda v: np.concatenate([v, v]).reshape(P, 1)
    rows = lambda v: np.broadcast_to(v.reshape(1, D), (P, D))
    half = HD // 2
    inv_freq = f(1.0) / f(10000.0) ** (np.arange(half, dtype=f) / f(half))
    angles = np.arange(SEQ, dtype=f)[:, None] * inv_freq[None, :]
    cos, sin = np.cos(angles).astype(f).T, np.sin(angles).astype(f).T
    cos = np.tile(np.concatenate([cos, cos]), (P // HD, NSEQ))
    sin = np.tile(np.concatenate([-sin, sin]), (P // HD, NSEQ))
    t = np.arange(SEQ)
    causal = np.where(t[None, :] > t[:, None], f(MASKED), f(0)).astype(f)
    return {"x": a["x"], "ctx": a["ctx_1024"], "wide": wide, "expert_down": expert_down, "latent_weights": lat,
            "gamma": twice(a["L0_attn_ln_gamma"]), "beta": twice(a["L0_attn_ln_beta"]),
            "b1": a["L0_xattn_b1"].reshape(KT, P).T, "b2": a["L0_xattn_b2"].reshape(KT, P).T,
            "b3": rows(a["L0_xattn_b3"]), "b4": rows(a["L0_xattn_b4"]),
            "rotary_table": np.concatenate([cos, sin], axis=1), "causal": causal, "causal_turned": causal.T}


def kernel(**inputs):
    import concourse.bacc as _bacc
    from concourse.bass_utils import run_bass_kernel_spmd as _run

    nc = _bacc.Bacc("TRN2", target_bir_lowering=False, num_devices=1)
    arrays, args = {}, []
    for name, a in _layout({k: np.asarray(v) for k, v in inputs.items()}).items():
        a = np.ascontiguousarray(a)
        arrays[f"in_{name}"] = a
        args.append(nc.dram_tensor(f"in_{name}", a.shape, mybir.dt.from_np(a.dtype), kind="ExternalInput").ap())
    out = nc.dram_tensor("out_x", (BATCH, SEQ, D), F32, kind="ExternalOutput").ap()
    decoder_layer(nc, *args, out)
    r = _run(nc, [arrays], core_ids=[0])
    return r.results[0]["out_x"]
```

```python
from contextlib import ExitStack

import numpy as np

import concourse.bass as bass
from concourse import mybir

F32 = mybir.dt.float32
F16 = mybir.dt.float16
BF16 = mybir.dt.bfloat16
ALU = mybir.AluOpType
ACT = mybir.ActivationFunctionType
AX_X = mybir.AxisListType.X

P = 128
BATCH, SEQ, D = 128, 128, 256
HEADS, HD = 16, 16
LATENT = 64
EXPERTS, TOP_K = 8, 2
SHARED_TILES = 2
TILES = SHARED_TILES + EXPERTS
NSEQ = 2
T = NSEQ * SEQ
NBLOCKS = BATCH // NSEQ
KT = D // P
HG = 4
GROUPS = HEADS // HG
PAIRS = HEADS // 2
VW = 32
EPS = 1e-5
WS = 16.0
SCORE_SCALE = 1.0 / (HD ** 0.5) / (WS * WS)
MASKED = -1e30
LOWEST = -3e38

SELF_IN, SELF_OUT, CROSS_IN, CROSS_OUT, FFN = range(5)
STAGES = (SELF_IN, SELF_OUT, CROSS_IN, CROSS_OUT, FFN)
ITERATIONS = NBLOCKS + len(STAGES) - 1
LOOP_FROM = 6
LOOP_TO = NBLOCKS - 2

WIDE = {}
_at = 0
for _name, _n in (("q", D), ("down_latent", LATENT), ("self_out", D), ("cross_q", D),
                  ("cross_k", D), ("cross_v", D), ("cross_out", D), ("shared_gate", D), ("shared_up", D),
                  ("shared_down", D), ("router", EXPERTS), ("gate", EXPERTS * P), ("up", EXPERTS * P)):
    WIDE[_name] = _at
    _at += _n
WIDE_COLS = _at
LAT = {"k": 0, "v": D}
LAT_COLS = 2 * D
CHUNK = 1024



def attention_chain(z):
    steps = []
    for s in range(NSEQ):
        for g in range(GROUPS):
            n = s * GROUPS + g
            steps += [(z, "scores", n), (z, "top", n)]
            if z == SELF_OUT:
                steps.append((z, "mask", n))
        for g in range(GROUPS):
            n = s * GROUPS + g
            steps += [(z, "weights", n), (z, "exp", n)]
            if g:
                steps.append((z, "values", n - 1))
        steps += [(z, "values", s * GROUPS + GROUPS - 1), (z, "out_copy", s), (z, "out_turn", s), (z, "divide", s)]
    return steps + [(z, kind, 0) for kind in ("feature_turn", "feature_hi", "feature_lo", "project", "residual")]


def ffn_chain():
    steps = [(FFN, kind, 0) for kind in (
        "moments", "rstd", "normalise", "norm_turn", "norm_hi", "norm_lo", "router", "gate", "rank", "router_exp",
        "up", "tanh", "product", "choose", "coef_turn", "coef_copy", "coef_spread")]
    for n in range(TILES):
        more = n + 1 < TILES
        steps += [(FFN, "gate", n + 1)] * more + [(FFN, "split_hi", n), (FFN, "split_lo", n)]
        steps += [(FFN, "up", n + 1), (FFN, "tanh", n + 1), (FFN, "product", n + 1)] * more
        steps += [(FFN, "down", n)]
    return steps + [(FFN, "result", 0), (FFN, "store", 0)]


def input_chain():
    steps = [(SELF_IN, kind, 0) for kind in ("moments", "rstd", "normalise", "norm_turn", "norm_hi", "norm_lo")]

    steps += [(SELF_IN, kind, 0) for kind in (
        "rotary", "rotary_mul", "rotary_add", "latent", "latent_moments", "latent_rstd", "rotary_hi", "rotary_lo",
        "latent_normalise", "latent_turn", "latent_hi", "latent_lo")]
    steps += [(SELF_IN, kind, 1) for kind in ("rotary", "rotary_mul", "rotary_add", "rotary_hi", "rotary_lo")]
    steps += [(SELF_IN, kind, 0) for kind in ("pack", "latent_values", "values_copy")]
    return steps + [(CROSS_IN, kind, 0) for kind in (
        "moments", "rstd", "context_hi", "add_b4", "context_lo", "normalise", "keys", "keys_hi", "keys_lo",
        "norm_turn", "norm_hi", "norm_lo", "queries", "queries_hi", "queries_lo", "pack", "context_values",
        "values_add")]


CHAINS = {"I": input_chain(), "S": attention_chain(SELF_OUT), "C": attention_chain(CROSS_OUT), "F": ffn_chain()}


def merged(order):
    left = {k: iter(v) for k, v in CHAINS.items()}
    assert all(order.count(k) == len(v) for k, v in CHAINS.items())
    return [next(left[k]) for k in order]


FILL_ORDER = (
    "ISISFSSIISCCSSSCFFIFFFFCFFSIFSFFSCFISCIFFSFSIFFCFFFFFISFCCFFFIFIFFSFFFFCSCISFIICCICF"
    "SSIFSFCISSFCICFFSCCCSSCFICIIIIFIIISFCCICFIISFCFFSISFSFCCSFCFSSSFSCSCSFCFCSFIFIFISCIS"
    "FCCSISFCISSICCFSFFCCIIFCFFCSSFCFSSCSFISFFFCFCFSFSFFCFICFIFFFISSSCFCFSSF")
LOOP_ORDER = (
    "SSSSCFSIFFISSSSFSFIISFISSFSFSCIFFFSSFSSFSCIFFFSFSCSIFCFCFIIFIFCFSFIFSSICICFCFFISSISS"
    "FICFCICFFCSIFCSCCFCSIFISCSFCFFCSFFSSCCFCICFIFSFSFSFCFFCFIFFISCFIFSFSCSCFIFSIIIFSCIIS"
    "FCSFCSCSCIFSFFFIIFFCCFFICFSCICCCFFFCSIFIICSSFFFFCIFIIFSCCSFCICFFCSFCFFF")
DRAIN_ORDER = (
    "SSSFSCFISSSIFIIIICFFSFCSSFFSCSFSIIFIFSFIIIISSCISFFIISCIFFIISSFFFIFSSIFSCSFFSIFFCFIFF"
    "CIFFFCFIFFSICISFSCCCSIFFFIFCICSFCSFIFCSCSIFFCFSFCFCFSCCSFSFSCSIIFSFCFCSFFIFFCSCSFSFC"
    "FIFSFFSSFCCCSFFSICCCSFICFCFIISCFCSIFCICFFCSSFCFCFFSCSCFSICFCSSFCFICFFFF")
FILL_STEPS, LOOP_STEPS, DRAIN_STEPS = merged(FILL_ORDER), merged(LOOP_ORDER), merged(DRAIN_ORDER)


class Signal:

    def __init__(self, sem, stage, per_block=1, unit=1):
        self.sem, self.stage, self.per_block, self.unit = sem, stage, per_block, unit

    def at(self, i, n=None):
        n = self.per_block if n is None else n
        return ((i - self.stage) * self.per_block + n) * self.unit

    def begun(self, i, n=None):
        value = self.at(i, n)
        return not isinstance(value, int) or value > 0


def decoder_layer(nc, x, ctxT, wide, expert_down, latent_weights, gamma, beta, b1, b2, b3, b4,
                  rotary_table, causal, out):
    ctx_stack = ExitStack()
    with ctx_stack:
        def sb(name, shape, dt):
            return ctx_stack.enter_context(nc.sbuf_tensor(name, shape, dt))

        def bank(name, shape=(P, 512)):
            return ctx_stack.enter_context(nc.psum_tensor(name, list(shape), F32))

        def sem(name):
            return ctx_stack.enter_context(nc.semaphore(name))

        def signal(name, stage, per_block=1, unit=1):
            return Signal(sem(name), stage, per_block, unit)

        wide_hi = sb("wide_hi", [P, KT, WIDE_COLS], F16)
        wide_lo = sb("wide_lo", [P, KT, WIDE_COLS], F16)
        down_hi = sb("down_hi", [P, EXPERTS * D], F16)
        down_lo = sb("down_lo", [P, EXPERTS * D], F16)
        lat_hi = sb("lat_hi", [P, LAT_COLS], F16)
        lat_lo = sb("lat_lo", [P, LAT_COLS], F16)
        gamma_sb = sb("gamma_sb", [P, 1], F32)
        gamma_scaled = sb("gamma_scaled", [P, 1], F32)
        beta_sb = sb("beta_sb", [P, 1], F32)
        b1_sb = sb("b1_sb", [P, KT], F32)
        b2_sb = sb("b2_sb", [P, KT], F32)
        b1_scaled = sb("b1_scaled", [P, KT], F32)
        b2_scaled = sb("b2_scaled", [P, KT], F32)
        b3_sb = sb("b3_sb", [P, D], F32)
        b4_sb = sb("b4_sb", [P, D], F32)
        rotary_sb = sb("rotary_sb", [P, 4, T], F32)
        causal_sb = sb("causal_sb", [P, SEQ], F32)
        causal_minus = sb("causal_minus", [P, SEQ], BF16)
        ident = sb("ident", [P, P], F32)
        minus_ident = sb("minus_ident", [P, P], BF16)
        earlier = sb("earlier", [P, EXPERTS, EXPERTS], F32)
        minus_half = sb("minus_half", [P, NSEQ], F32)

        NORMED = (SELF_IN, CROSS_IN, FFN)
        tag = {SELF_IN: "self", CROSS_IN: "cross", FFN: "ffn", SELF_OUT: "selfo", CROSS_OUT: "crosso"}
        stats = {z: sb(f"stats_{tag[z]}", [P, NSEQ, 6], F32) for z in NORMED}
        moments = {z: sb(f"moments_{tag[z]}", [P, NSEQ, 2], F32) for z in NORMED}
        variance = {z: sb(f"variance_{tag[z]}", [P, NSEQ], F32) for z in NORMED}
        rstd = {z: sb(f"rstd_{tag[z]}", [P, NSEQ], F32) for z in NORMED}
        x_in = sb("x_in", [P, NSEQ, D], F32)
        normed = {z: sb(f"normed_{tag[z]}", [P, NSEQ, D], F32) for z in (CROSS_IN, FFN)}
        normed[SELF_IN] = x_in
        xT_hi = {z: sb(f"xT_hi_{tag[z]}", [P, KT, T], F16) for z in NORMED}
        xT_lo = {z: sb(f"xT_lo_{tag[z]}", [P, KT, T], F16) for z in NORMED}

        wait_holder = sb("wait_holder", [P, 1], F32)

        rotary_parts = sb("rotary_parts", [P, 2, 2, T], F32)
        self_qk_hi = sb("self_qk_hi", [P, 4, T], F16)
        self_qk_lo = sb("self_qk_lo", [P, 4, T], F16)
        lat_stats = sb("lat_stats", [P, NSEQ, 6], F32)
        lat_moments = sb("lat_moments", [P, NSEQ, 2], F32)
        lat_variance = sb("lat_variance", [P, NSEQ], F32)
        lat_rstd = sb("lat_rstd", [P, NSEQ], F32)
        lat_twice = sb("lat_twice", [P, NSEQ, 2, LATENT], F32)
        latT = sb("latT", [P, T], F32)
        latT_split = sb("latT_split", [P, T], F16)

        ctxT_in = sb("ctxT_in", [P, KT, T], F32)
        ctxT_hi = sb("ctxT_hi", [P, KT, T], F16)
        ctxT_lo = sb("ctxT_lo", [P, KT, T], F16)
        cross_qk_hi = sb("cross_qk_hi", [P, 4, T], F16)
        cross_qk_lo = sb("cross_qk_lo", [P, 4, T], F16)

        ATT = (SELF_OUT, CROSS_OUT)
        q_packed = {z: [sb(f"q_packed_{tag[z]}{h}", [P, HEADS, T], F16) for h in range(2)] for z in ATT}
        k_packed = {z: [sb(f"k_packed_{tag[z]}{h}", [P, PAIRS, T], F16) for h in range(2)] for z in ATT}
        values = {z: [sb(f"values_{tag[z]}{h}", [P, NSEQ, HEADS, VW], F32) for h in range(2)] for z in ATT}
        probs = {z: sb(f"probs_{tag[z]}", [P, HEADS, SEQ], F32) for z in ATT}
        top_score = {z: sb(f"top_score_{tag[z]}", [P, NSEQ, HEADS], F32 if z == SELF_OUT else BF16) for z in ATT}
        masked_scores = sb("masked_scores", [P, HG, SEQ], BF16)
        top_masked = sb("top_masked", [P, HEADS, SEQ], BF16)
        outT = {z: sb(f"outT_{tag[z]}", [P, HG * SEQ], F32) for z in ATT}
        inverse = {z: sb(f"inverse_{tag[z]}", [P, HEADS], F32) for z in ATT}
        heads_out = {z: sb(f"heads_out_{tag[z]}", [P, NSEQ, D], F32) for z in ATT}
        headsT_hi = {z: sb(f"headsT_hi_{tag[z]}", [P, KT, T], F16) for z in ATT}
        headsT_lo = {z: sb(f"headsT_lo_{tag[z]}", [P, KT, T], F16) for z in ATT}
        x_again = sb("x_again", [P, NSEQ, D], F32)
        x1 = [sb(f"x1_{h}", [P, NSEQ, D], F32) for h in range(2)]
        x1_b4 = [sb(f"x1_b4_{h}", [P, NSEQ, D], F32) for h in range(2)]
        x2 = [sb(f"x2_{h}", [P, NSEQ, D], F32) for h in range(2)]

        logits = sb("logits", [P, NSEQ, EXPERTS], F32)
        top_logit = sb("top_logit", [P, NSEQ], F32)
        shifted = sb("shifted", [P, NSEQ, EXPERTS], F32)
        exps = sb("exps", [P, NSEQ, EXPERTS], F32)
        exp_sum = sb("exp_sum", [P, NSEQ], F32)
        exp_inv = sb("exp_inv", [P, NSEQ], F32)
        router_probs = sb("router_probs", [P, NSEQ, EXPERTS], F32)
        greater = sb("greater", [P, NSEQ, EXPERTS, EXPERTS], BF16)
        equal = sb("equal", [P, NSEQ, EXPERTS, EXPERTS], BF16)
        rank = sb("rank", [P, NSEQ, EXPERTS], F32)
        coef = sb("coef", [P, NSEQ, EXPERTS], F32)
        coefT = sb("coefT", [NSEQ * EXPERTS, SEQ], F32)
        coef_rows = sb("coef_rows", [P, 2, T], F32)
        tanh_sb = sb("tanh_sb", [P, T], F32)
        gated = sb("gated", [P, T], F32)
        hidden = sb("hidden", [P, T], F32)
        hidden_c = sb("hidden_c", [P, 2, T], F32)
        hidden_hi = sb("hidden_hi", [P, 2, T], F16)
        hidden_lo = sb("hidden_lo", [P, 2, T], F16)
        result = sb("result", [P, NSEQ, D], F32)

        setup_bank = bank("setup_bank")
        score_bank = {z: bank(f"score_bank_{tag[z]}") for z in ATT}
        out_bank = {z: bank(f"out_bank_{tag[z]}") for z in ATT}
        gate_up_bank = [bank("gate_up_bank0"), bank("gate_up_bank1")]
        down_bank = bank("down_bank")

        scratch = {z: nc.dram_tensor(f"qk_scratch_{tag[z]}", [2, 4, P, T], F16, kind="Internal").ap()
                   for z in ATT}
        coef_scratch = nc.dram_tensor("coef_scratch", [NSEQ, EXPERTS, SEQ], F32, kind="Internal").ap()

        constants_loaded = sem("constants_loaded")
        chunk_loaded = [sem(f"chunk_loaded{k}") for k in range(4)]
        chunk_hi = sem("chunk_hi")
        chunk_lo = sem("chunk_lo")
        pool_ready = sem("pool_ready")
        ident_ready = sem("ident_ready")
        padding_ready = sem("padding_ready")
        act_ready = sem("act_ready")
        dve_ready = sem("dve_ready")

        norm_steps = {z: signal(f"norm_steps_{tag[z]}", z, 3) for z in NORMED}
        rstd_done = {z: signal(f"rstd_done_{tag[z]}", z) for z in NORMED}
        norm_done = {z: signal(f"norm_done_{tag[z]}", z) for z in NORMED}
        norm_turned = {z: signal(f"norm_turned_{tag[z]}", z) for z in NORMED}
        xT_hi_done = {z: signal(f"xT_hi_done_{tag[z]}", z) for z in NORMED}
        xT_lo_done = {z: signal(f"xT_lo_done_{tag[z]}", z) for z in NORMED}

        x_loaded = signal("x_loaded", SELF_IN, 1, 16)
        rotary_projected = signal("rotary_projected", SELF_IN, 2)
        rotary_multiplied = signal("rotary_multiplied", SELF_IN, 2)
        rotary_added = signal("rotary_added", SELF_IN, 2)
        rotary_hi_done = signal("rotary_hi_done", SELF_IN, 2)
        rotary_lo_done = signal("rotary_lo_done", SELF_IN, 2)
        latent_projected = signal("latent_projected", SELF_IN)
        latent_steps = signal("latent_steps", SELF_IN, 3)
        latent_rstd = signal("latent_rstd", SELF_IN)
        latent_normed = signal("latent_normed", SELF_IN)
        latent_turned = signal("latent_turned", SELF_IN)
        latent_affine = signal("latent_affine", SELF_IN)
        latent_hi_done = signal("latent_hi_done", SELF_IN)
        latent_split = signal("latent_split", SELF_IN)
        values_projected = {SELF_OUT: signal("self_values_projected", SELF_IN),
                            CROSS_OUT: signal("cross_values_projected", CROSS_IN)}
        values_ready = {SELF_OUT: signal("self_values_ready", SELF_IN),
                        CROSS_OUT: signal("cross_values_ready", CROSS_IN)}
        qk_stored = {SELF_OUT: signal("self_qk_stored", SELF_IN, 2, 16),
                     CROSS_OUT: signal("cross_qk_stored", CROSS_IN, 2, 16)}
        qk_packed = {SELF_OUT: signal("self_qk_packed", SELF_IN, 12, 16),
                     CROSS_OUT: signal("cross_qk_packed", CROSS_IN, 12, 16)}

        ctx_loaded = signal("ctx_loaded", CROSS_IN, KT, 16)
        ctx_hi_done = signal("ctx_hi_done", CROSS_IN)
        ctx_lo_done = signal("ctx_lo_done", CROSS_IN)
        qk_projected = signal("qk_projected", CROSS_IN, 2)
        qk_hi_done = signal("qk_hi_done", CROSS_IN, 2)
        qk_lo_done = signal("qk_lo_done", CROSS_IN, 2)
        x1_b4_done = signal("x1_b4_done", CROSS_IN)

        NG = NSEQ * GROUPS
        scored = {z: signal(f"scored_{tag[z]}", z, NG) for z in ATT}
        maxed = {z: signal(f"maxed_{tag[z]}", z, NG) for z in ATT}
        top_masked_done = signal("top_masked_done", SELF_OUT, NG)
        weighed = {z: signal(f"weighed_{tag[z]}", z, NG) for z in ATT}
        exped = {z: signal(f"exped_{tag[z]}", z, NG) for z in ATT}
        valued = {z: signal(f"valued_{tag[z]}", z, NG) for z in ATT}
        out_copied = {z: signal(f"out_copied_{tag[z]}", z, NSEQ) for z in ATT}
        out_turned = {z: signal(f"out_turned_{tag[z]}", z, NSEQ) for z in ATT}
        inverted = {z: signal(f"inverted_{tag[z]}", z, NSEQ) for z in ATT}
        divided = {z: signal(f"divided_{tag[z]}", z, NSEQ) for z in ATT}
        heads_turned = {z: signal(f"heads_turned_{tag[z]}", z) for z in ATT}
        heads_hi_done = {z: signal(f"heads_hi_done_{tag[z]}", z) for z in ATT}
        heads_lo_done = {z: signal(f"heads_lo_done_{tag[z]}", z) for z in ATT}
        projected = {z: signal(f"projected_{tag[z]}", z) for z in ATT}
        residual_added = {z: signal(f"residual_added_{tag[z]}", z) for z in ATT}
        x_again_loaded = signal("x_again_loaded", SELF_OUT, 1, 16)

        routed = signal("routed", FFN)
        choose_steps = signal("choose_steps", FFN, 11)
        router_exped = signal("router_exped", FFN)
        gate_up_done = signal("gate_up_done", FFN, TILES)
        coef_turned = signal("coef_turned", FFN)
        coef_copied = signal("coef_copied", FFN)
        coef_stored = signal("coef_stored", FFN, 1, 16)
        coef_spread = [signal(f"coef_spread{k}", FFN, EXPERTS // 2, 16) for k in range(2)]
        tanh_done = signal("tanh_done", FFN, TILES)
        gated_done = signal("gated_done", FFN, TILES)
        hidden_done = signal("hidden_done", FFN, TILES)
        hidden_scaled = signal("hidden_scaled", FFN, EXPERTS)
        hidden_hi_done = signal("hidden_hi_done", FFN, TILES)
        hidden_lo_done = signal("hidden_lo_done", FFN, TILES)
        down_done = signal("down_done", FFN, TILES)
        result_done = signal("result_done", FFN)
        result_stored = signal("result_stored", FFN, 1, 16)

        def w(name, kt, c0, n):
            a = WIDE[name] + c0
            return wide_hi[:, kt, a:a + n], wide_lo[:, kt, a:a + n]

        chunks = []
        for c in range(0, WIDE_COLS, CHUNK):
            e = min(c + CHUNK, WIDE_COLS)
            for kt in range(KT):
                chunks.append((wide[kt * P:(kt + 1) * P, c:e], wide_hi[:, kt, c:e], wide_lo[:, kt, c:e]))
            if c == 0:
                chunks.append((latent_weights, lat_hi[:, :], lat_lo[:, :]))
                FIRST_CHUNKS = len(chunks)
        for c in range(0, EXPERTS * D, CHUNK):
            chunks.append((expert_down[:, c:c + CHUNK], down_hi[:, c:c + CHUNK], down_lo[:, c:c + CHUNK]))
        staging = [probs[z][:, :, :].rearrange("p h q -> p (h q)")[:, k * CHUNK:(k + 1) * CHUNK]
                   for z in ATT for k in range(2)]
        STAGED = len(staging)

        def slot_of(i_parity, stage):
            return (i_parity + stage) % 2

        def run(eng, body, after_first=None):
            def active(i):
                return [z for z in STAGES if 0 <= i - z < NBLOCKS]
            def steps(i):
                return FILL_STEPS if i < len(STAGES) - 1 else LOOP_STEPS if i < NBLOCKS else DRAIN_STEPS
            for i in range(LOOP_FROM):
                body(i, i % 2, active(i), steps(i))
                if i == 0 and after_first:
                    after_first()
            with eng.Fori(LOOP_FROM, LOOP_TO, 2) as i:
                body(i, 0, list(STAGES), LOOP_STEPS)
                body(i + 1, 1, list(STAGES), LOOP_STEPS)
            for i in range(LOOP_TO, ITERATIONS):
                body(i, i % 2, active(i), steps(i))

        block = ctx_stack.enter_context(nc.Block())

        @block.sync
        def _(sp):
            def rows(tensor, b):
                return tensor[bass.ds(b * NSEQ, NSEQ)].rearrange("s t d -> t s d")

            def load_x(i):
                if norm_turned[SELF_IN].begun(i - 1):
                    sp.wait_ge(norm_turned[SELF_IN].sem, norm_turned[SELF_IN].at(i - 1))
                sp.dma_start(x_in[:, :, :], rows(x, i)).then_inc(x_loaded.sem, 16)

            def load_ctx(i):
                if ctx_lo_done.begun(i - 1):
                    sp.wait_ge(ctx_lo_done.sem, ctx_lo_done.at(i - 1))
                for kt in range(KT):
                    src = ctxT[bass.ds((i - CROSS_IN) * NSEQ, NSEQ), kt * P:(kt + 1) * P].rearrange("s d t -> d s t")
                    sp.dma_start(ctxT_in[:, kt, :].rearrange("d (s t) -> d s t", s=NSEQ),
                                 src).then_inc(ctx_loaded.sem, 16)

            def by_row(z, part):
                if z == SELF_OUT:
                    return scratch[z][part].rearrange("(q m) (r a) t -> (m r) q (a t)", q=2, a=2)
                return scratch[z][part].rearrange("m p t -> p m t")

            def pack(i, parity, z, hi, lo, hi_done, lo_done):
                half = slot_of(parity, z - 1)
                if isinstance(i, int) and i in (1, CROSS_IN):
                    sp.wait_ge(padding_ready, 4)
                sp.wait_ge(hi_done.sem, hi_done.at(i))
                if qk_packed[z].begun(i - 1):
                    sp.wait_ge(qk_packed[z].sem, qk_packed[z].at(i - 1))
                sp.dma_start(by_row(z, 0), hi[:, :, :]).then_inc(qk_stored[z].sem, 16)
                sp.wait_ge(lo_done.sem, lo_done.at(i))
                sp.dma_start(by_row(z, 1), lo[:, :, :]).then_inc(qk_stored[z].sem, 16)
                sp.wait_ge(qk_stored[z].sem, qk_stored[z].at(i))
                for c in range(4):
                    keys = scratch[z][c % 2, 2:4].rearrange("m (j r) t -> r (m j) t", r=32)
                    sp.dma_start(k_packed[z][half][32 * c:32 * c + 32, :, :], keys).then_inc(qk_packed[z].sem, 16)
                    for odd in range(2):
                        r = 32 * c + 16 * odd
                        queries = scratch[z][c // 2, 0:2].rearrange("m (j o d) t -> o d (m j) t", o=2, d=HD)[odd]
                        dst = q_packed[z][half][r:r + HD, :, :].rearrange("d (j o) t -> d o j t", o=2)[:, odd]
                        sp.dma_start(dst, queries).then_inc(qk_packed[z].sem, 16)

            def spread(i, e):
                sp.dma_start(coef_rows[:, e % 2, :].rearrange("p (s t) -> p s t", s=NSEQ),
                             coef_scratch[:, e, :].unsqueeze(0).to_broadcast([P, NSEQ, SEQ])
                             ).then_inc(coef_spread[e % 2].sem, 16)

            def body(i, parity, active, steps):
                load_ahead = not isinstance(i, int) or 0 <= i + 1 - CROSS_IN < NBLOCKS
                for z, kind, n in steps:
                    if z == SELF_IN and kind == "norm_hi" and (not isinstance(i, int) or i + 1 < NBLOCKS):
                        load_x(i + 1)
                    if z == CROSS_IN and kind == "norm_turn" and load_ahead:
                        load_ctx(i + 1)
                    if z not in active:
                        continue
                    if z == SELF_OUT and kind == "scores" and n == 0:
                        if residual_added[SELF_OUT].begun(i - 1):
                            sp.wait_ge(residual_added[SELF_OUT].sem, residual_added[SELF_OUT].at(i - 1))
                        sp.dma_start(x_again[:, :, :], rows(x, i - SELF_OUT)).then_inc(x_again_loaded.sem, 16)
                    if z == SELF_IN and kind == "pack":
                        pack(i, parity, SELF_OUT, self_qk_hi, self_qk_lo, rotary_hi_done, rotary_lo_done)
                    if z == CROSS_IN and kind == "pack":
                        pack(i, parity, CROSS_OUT, cross_qk_hi, cross_qk_lo, qk_hi_done, qk_lo_done)
                    if kind == "coef_spread":
                        sp.wait_ge(coef_copied.sem, coef_copied.at(i))
                        sp.dma_start(coef_scratch.rearrange("s e t -> (s e) t"),
                                     coefT[:, :]).then_inc(coef_stored.sem, 16)
                        sp.wait_ge(coef_stored.sem, coef_stored.at(i))
                        spread(i, 0)
                        spread(i, 1)
                    if kind == "product" and SHARED_TILES <= n < TILES - 2:
                        e = n - SHARED_TILES
                        sp.wait_ge(hidden_scaled.sem, hidden_scaled.at(i, e + 1))
                        spread(i, e + 2)
                    if kind == "store":
                        sp.wait_ge(result_done.sem, result_done.at(i))
                        sp.dma_start(rows(out, i - FFN), result[:, :, :]).then_inc(result_stored.sem, 16)

            def load_chunks(first, last):
                for n in range(first, last):
                    src, hi, _ = chunks[n]
                    if n >= STAGED:
                        sp.wait_ge(chunk_lo, n - STAGED + 1)
                    k = n % STAGED
                    sp.dma_start(staging[k][:, 0:src.shape[1]], src).then_inc(chunk_loaded[k], 16)

            load_chunks(0, FIRST_CHUNKS)
            load_x(0)
            for dst, src in ((gamma_sb[:, :], gamma), (beta_sb[:, :], beta), (b1_sb[:, :], b1),
                             (b2_sb[:, :], b2), (b3_sb[:, :], b3), (b4_sb[:, :], b4),
                             (rotary_sb[:, :, :].rearrange("p a t -> p (a t)"), rotary_table),
                             (causal_sb[:, :], causal)):
                sp.dma_start(dst, src).then_inc(constants_loaded, 16)
            load_chunks(FIRST_CHUNKS, len(chunks))
            sp.wait_ge(padding_ready, 1)
            run(sp, body)
            sp.wait_ge(result_stored.sem, result_stored.at(ITERATIONS - 1))
            sp.wait_ge(qk_packed[SELF_OUT].sem, qk_packed[SELF_OUT].at(NBLOCKS - 1 + SELF_IN))
            sp.wait_ge(qk_packed[CROSS_OUT].sem, qk_packed[CROSS_OUT].at(NBLOCKS - 1 + CROSS_IN))

        @block.gpsimd
        def _(pool):
            nc.gpsimd.memset(ident[:, :], 0.0)
            nc.gpsimd.memset(earlier[:, :, :], 1.0)
            nc.gpsimd.memset(minus_half[:, :], -0.5).then_inc(ident_ready, 1)
            pool.wait_ge(ident_ready, 1)
            nc.gpsimd.affine_select(out=ident[:, :], in_=ident[:, :], compare_op=ALU.not_equal, fill=1.0,
                                    base=0, pattern=[[-1, P]], channel_multiplier=1)
            nc.gpsimd.affine_select(out=earlier[:, :, :], in_=earlier[:, :, :], compare_op=ALU.is_gt,
                                    fill=0.0, base=0, pattern=[[1, EXPERTS], [-1, EXPERTS]],
                                    channel_multiplier=0).then_inc(pool_ready, 1)

            def pad(z, half):
                nc.gpsimd.memset(q_packed[z][half][:, :, :].bitcast(F32), 0.0)
                nc.gpsimd.memset(values[z][half][:, :, :, :], 1.0).then_inc(padding_ready, 1)

            pad(SELF_OUT, 0)

            def body(i, parity, active, steps):
                for z, kind, n in steps:
                    if z not in active:
                        continue
                    if kind == "rstd":
                        pool.wait_ge(norm_steps[z].sem, norm_steps[z].at(i))
                        nc.gpsimd.tensor_tensor(rstd[z][:, :], variance[z][:, :], minus_half[:, :],
                                                ALU.pow).then_inc(rstd_done[z].sem, 1)
                    if kind == "add_b4":
                        pool.wait_ge(residual_added[SELF_OUT].sem, residual_added[SELF_OUT].at(i - 1))
                        if residual_added[CROSS_OUT].begun(i - 1):
                            pool.wait_ge(residual_added[CROSS_OUT].sem, residual_added[CROSS_OUT].at(i - 1))
                        h = slot_of(parity, z)
                        nc.gpsimd.tensor_tensor(x1_b4[h][:, :, :], x1[h][:, :, :],
                                                b4_sb[:, :].unsqueeze(1).to_broadcast([P, NSEQ, D]),
                                                ALU.add).then_inc(x1_b4_done.sem, 1)
                    if kind == "context_lo":
                        pool.wait_ge(ctx_hi_done.sem, ctx_hi_done.at(i))
                        nc.gpsimd.tensor_tensor(ctxT_lo[:, :, :], ctxT_in[:, :, :], ctxT_hi[:, :, :],
                                                ALU.subtract).then_inc(ctx_lo_done.sem, 1)
                    if kind == "mask":
                        pool.wait_ge(maxed[z].sem, maxed[z].at(i, n + 1))
                        s, g = divmod(n, GROUPS)
                        heads = slice(g * HG, (g + 1) * HG)
                        nc.gpsimd.tensor_tensor(top_masked[:, heads, :],
                                                top_score[z][:, s, heads].unsqueeze(2).to_broadcast([P, HG, SEQ]),
                                                causal_minus[:, :].unsqueeze(1).to_broadcast([P, HG, SEQ]),
                                                ALU.add).then_inc(top_masked_done.sem, 1)
                    if kind == "latent_rstd":
                        pool.wait_ge(latent_steps.sem, latent_steps.at(i))
                        nc.gpsimd.tensor_tensor(lat_rstd[:, :], lat_variance[:, :], minus_half[:, :],
                                                ALU.pow).then_inc(latent_rstd.sem, 1)
                    if kind == "rotary_add":
                        pool.wait_ge(rotary_multiplied.sem, rotary_multiplied.at(i, n + 1))
                        nc.gpsimd.tensor_tensor(rotary_parts[:, :, 0, :], rotary_parts[:, :, 0, :],
                                                rotary_parts[:, :, 1, :], ALU.add).then_inc(rotary_added.sem, 1)
                    if kind == "rotary_lo":
                        pool.wait_ge(rotary_hi_done.sem, rotary_hi_done.at(i, n + 1))
                        if n == 0:
                            if qk_stored[SELF_OUT].begun(i - 1):
                                pool.wait_ge(qk_stored[SELF_OUT].sem, qk_stored[SELF_OUT].at(i - 1))
                        nc.gpsimd.tensor_tensor(self_qk_lo[:, 2 * n:2 * n + 2, :], rotary_parts[:, :, 0, :],
                                                self_qk_hi[:, 2 * n:2 * n + 2, :],
                                                ALU.subtract).then_inc(rotary_lo_done.sem, 1)
                    if kind == "split_lo":
                        pool.wait_ge(hidden_hi_done.sem, hidden_hi_done.at(i, n + 1))
                        nc.gpsimd.tensor_tensor(hidden_lo[:, n % 2, :], hidden_c[:, n % 2, :], hidden_hi[:, n % 2, :],
                                                ALU.subtract).then_inc(hidden_lo_done.sem, 1)

            run(pool, body, lambda: [pad(SELF_OUT, 1), pad(CROSS_OUT, 0), pad(CROSS_OUT, 1)])

        @block.scalar
        def _(act):
            def split_heads(first, last):
                for n in range(first, last):
                    src, hi, _ = chunks[n]
                    act.wait_ge(chunk_loaded[n % STAGED], 16 * (n // STAGED + 1))
                    nc.scalar.mul(hi, staging[n % STAGED][:, 0:src.shape[1]], WS).then_inc(chunk_hi, 1)

            def other_weights():
                split_heads(FIRST_CHUNKS, len(chunks))
                act.wait_ge(chunk_lo, len(chunks))

            split_heads(0, FIRST_CHUNKS)
            act.wait_ge(pool_ready, 1)
            nc.scalar.mul(minus_ident[:, :], ident[:, :], -1.0)
            act.wait_ge(constants_loaded, 16 * 8)
            nc.scalar.mul(gamma_scaled[:, :], gamma_sb[:, :], 1.0 / WS)
            nc.scalar.mul(b1_scaled[:, :], b1_sb[:, :], WS)
            nc.scalar.mul(b2_scaled[:, :], b2_sb[:, :], WS)
            nc.scalar.mul(causal_minus[:, :], causal_sb[:, :], -1.0).then_inc(act_ready, 1)
            act.wait_ge(act_ready, 1)

            def body(i, parity, active, steps):
                for z, kind, n in steps:
                    if z not in active:
                        continue
                    if kind == "norm_hi":
                        act.wait_ge(norm_turned[z].sem, norm_turned[z].at(i))
                        src = gate_up_bank[1] if z == FFN else setup_bank
                        nc.scalar.copy(xT_hi[z][:, :, :].rearrange("p k t -> p (k t)"),
                                       src[:, :]).then_inc(xT_hi_done[z].sem, 1)
                    if kind == "rotary_hi":
                        act.wait_ge(rotary_added.sem, rotary_added.at(i, n + 1))
                        if n == 0:
                            if qk_stored[SELF_OUT].begun(i - 1):
                                act.wait_ge(qk_stored[SELF_OUT].sem, qk_stored[SELF_OUT].at(i - 1))
                        nc.scalar.copy(self_qk_hi[:, 2 * n:2 * n + 2, :],
                                       rotary_parts[:, :, 0, :]).then_inc(rotary_hi_done.sem, 1)
                    if kind == "latent_hi":
                        act.wait_ge(latent_turned.sem, latent_turned.at(i))
                        if latent_split.begun(i - 1):
                            act.wait_ge(latent_split.sem, latent_split.at(i - 1))
                        nc.scalar.activation(latT[:, :], setup_bank[:, 0:T], ACT.Identity, bias=beta_sb[:, 0:1],
                                             scale=gamma_scaled[:, 0:1]).then_inc(latent_affine.sem, 1)
                        act.wait_ge(latent_affine.sem, latent_affine.at(i))
                        nc.scalar.copy(latT_split[:, :], latT[:, :]).then_inc(latent_hi_done.sem, 1)
                    if kind == "values_copy":
                        act.wait_ge(values_projected[SELF_OUT].sem, values_projected[SELF_OUT].at(i))
                        if isinstance(i, int) and i < 2:
                            act.wait_ge(padding_ready, 1 + 3 * i)
                        h = slot_of(parity, SELF_IN)
                        nc.scalar.mul(values[SELF_OUT][h][:, :, :, 0:HD],
                                      setup_bank[:, :].rearrange("p (s h d) -> p s h d", s=NSEQ, h=HEADS),
                                      1.0 / WS).then_inc(values_ready[SELF_OUT].sem, 1)
                    if kind == "context_hi":
                        act.wait_ge(ctx_loaded.sem, ctx_loaded.at(i))
                        if values_projected[CROSS_OUT].begun(i - 1):
                            act.wait_ge(values_projected[CROSS_OUT].sem, values_projected[CROSS_OUT].at(i - 1))
                        nc.scalar.copy(ctxT_hi[:, :, :], ctxT_in[:, :, :]).then_inc(ctx_hi_done.sem, 1)
                    if kind in ("keys_hi", "queries_hi"):
                        m0, bias, k = (2, b2_scaled, 1) if kind == "keys_hi" else (0, b1_scaled, 2)
                        act.wait_ge(qk_projected.sem, qk_projected.at(i, k))
                        if kind == "keys_hi":
                            if qk_stored[CROSS_OUT].begun(i - 1):
                                act.wait_ge(qk_stored[CROSS_OUT].sem, qk_stored[CROSS_OUT].at(i - 1))
                        for m in range(KT):
                            last = nc.scalar.activation(cross_qk_hi[:, m0 + m, :], setup_bank[:, m * T:(m + 1) * T],
                                                        ACT.Identity, bias=bias[:, m:m + 1])
                        last.then_inc(qk_hi_done.sem, 1)
                    if kind == "exp":
                        act.wait_ge(weighed[z].sem, weighed[z].at(i, n + 1))
                        g = n % GROUPS
                        nc.scalar.activation(probs[z][:, g * HG:(g + 1) * HG, :],
                                             score_bank[z][:, :].rearrange("p (h q) -> p h q", h=HG), ACT.Exp,
                                             scale=SCORE_SCALE).then_inc(exped[z].sem, 1)
                    if kind == "out_copy":
                        act.wait_ge(valued[z].sem, valued[z].at(i, (n + 1) * GROUPS))
                        nc.scalar.copy(outT[z][:, :], out_bank[z][:, :]).then_inc(out_copied[z].sem, 1)
                    if kind == "feature_hi":
                        act.wait_ge(heads_turned[z].sem, heads_turned[z].at(i))
                        nc.scalar.copy(headsT_hi[z][:, :, :].rearrange("p k t -> p (k t)"),
                                       out_bank[z][:, :]).then_inc(heads_hi_done[z].sem, 1)
                    if kind == "router_exp":
                        act.wait_ge(choose_steps.sem, choose_steps.at(i, 3))
                        nc.scalar.activation(exps[:, :, :], shifted[:, :, :], ACT.Exp).then_inc(router_exped.sem, 1)
                    if kind == "tanh":
                        act.wait_ge(gate_up_done.sem, gate_up_done.at(i, n + 1))
                        nc.scalar.activation(tanh_sb[:, :], gate_up_bank[n % 2][:, 0:T], ACT.Tanh,
                                             scale=0.5 / WS).then_inc(tanh_done.sem, 1)
                    if kind == "coef_copy":
                        act.wait_ge(coef_turned.sem, coef_turned.at(i))
                        if coef_stored.begun(i - 1):
                            act.wait_ge(coef_stored.sem, coef_stored.at(i - 1))
                        nc.scalar.copy(coefT[:, :],
                                       gate_up_bank[1][0:NSEQ * EXPERTS, 0:SEQ]).then_inc(coef_copied.sem, 1)
                    if kind == "split_hi":
                        act.wait_ge(hidden_done.sem, hidden_done.at(i, n + 1))
                        if n >= SHARED_TILES:
                            act.wait_ge(hidden_scaled.sem, hidden_scaled.at(i, n - SHARED_TILES + 1))
                        nc.scalar.copy(hidden_hi[:, n % 2, :], hidden_c[:, n % 2, :]).then_inc(hidden_hi_done.sem, 1)

            run(act, body, other_weights)

        @block.vector
        def _(dve):
            def split_remainders(first, last):
                for n in range(first, last):
                    src, hi, lo = chunks[n]
                    dve.wait_ge(chunk_hi, n + 1)
                    nc.vector.scalar_tensor_tensor(out=lo, in0=staging[n % STAGED][:, 0:src.shape[1]], scalar=WS,
                                                   in1=hi, op0=ALU.mult, op1=ALU.subtract).then_inc(chunk_lo, 1)

            split_remainders(0, FIRST_CHUNKS)

            def norm_source(parity, z):
                return {SELF_IN: x_in, CROSS_IN: x1[slot_of(parity, CROSS_IN)], FFN: x2[slot_of(parity, FFN)]}[z]

            def measure(i, parity, z):
                src = norm_source(parity, z)
                if z == SELF_IN:
                    dve.wait_ge(x_loaded.sem, x_loaded.at(i))
                if z == CROSS_IN:
                    if residual_added[SELF_OUT].begun(i - 1):
                        dve.wait_ge(residual_added[SELF_OUT].sem, residual_added[SELF_OUT].at(i - 1))
                if z == FFN:
                    if residual_added[CROSS_OUT].begun(i - 1):
                        dve.wait_ge(residual_added[CROSS_OUT].sem, residual_added[CROSS_OUT].at(i - 1))
                for s in range(NSEQ):
                    last = nc.vector.bn_stats(stats[z][:, s, :], src[:, s, :])
                last.then_inc(norm_steps[z].sem, 1)
                dve.wait_ge(norm_steps[z].sem, norm_steps[z].at(i, 1))
                nc.vector.memset(wait_holder[:, :], 0.0)
                for s in range(NSEQ):
                    last = nc.vector.bn_aggr(moments[z][:, s, :], stats[z][:, s, :])
                last.then_inc(norm_steps[z].sem, 1)
                dve.wait_ge(norm_steps[z].sem, norm_steps[z].at(i, 2))
                nc.vector.tensor_scalar(variance[z][:, :], moments[z][:, :, 1], EPS, None,
                                        ALU.add).then_inc(norm_steps[z].sem, 1)

            def normalise(i, parity, z):
                src = norm_source(parity, z)
                dve.wait_ge(rstd_done[z].sem, rstd_done[z].at(i))
                for s in range(NSEQ):
                    last = nc.vector.tensor_scalar(normed[z][:, s, :], src[:, s, :], moments[z][:, s, 0:1],
                                                   rstd[z][:, s:s + 1], ALU.subtract, ALU.mult)
                last.then_inc(norm_done[z].sem, 1)

            def remainder(lo, src, hi):
                return nc.vector.tensor_tensor(lo[:, :, :].rearrange("p k t -> p (k t)"), src[:, :],
                                               hi[:, :, :].rearrange("p k t -> p (k t)"), ALU.subtract)

            def step(i, n, instruction):
                instruction.then_inc(choose_steps.sem, 1)
                dve.wait_ge(choose_steps.sem, choose_steps.at(i, n))

            v = nc.vector
            pair = [P, NSEQ, EXPERTS]
            quad = [P, EXPERTS, EXPERTS]

            def rank_experts(i):
                dve.wait_ge(routed.sem, routed.at(i))
                step(i, 1, v.tensor_scalar(logits[:, :, :], gate_up_bank[1][:, 0:NSEQ * EXPERTS].rearrange(
                    "p (s e) -> p s e", s=NSEQ), 1.0 / WS, None, ALU.mult))
                step(i, 2, v.reduce_max(top_logit[:, :], logits[:, :, :], AX_X))
                step(i, 3, v.tensor_tensor(shifted[:, :, :], logits[:, :, :],
                                        top_logit[:, :].unsqueeze(2).to_broadcast(pair), ALU.subtract))
                for s in range(NSEQ):
                    mine = logits[:, s, :].unsqueeze(2).to_broadcast(quad)
                    other = logits[:, s, :].unsqueeze(1).to_broadcast(quad)
                    v.tensor_tensor(greater[:, s, :, :], other, mine, ALU.is_gt)
                    last = v.tensor_tensor(equal[:, s, :, :], other, mine, ALU.is_equal)
                step(i, 4, last)
                for s in range(NSEQ):
                    last = v.tensor_tensor(equal[:, s, :, :], equal[:, s, :, :], earlier[:, :, :], ALU.mult)
                step(i, 5, last)
                step(i, 6, v.tensor_tensor(greater[:, :, :, :], greater[:, :, :, :], equal[:, :, :, :], ALU.add))
                step(i, 7, v.reduce_sum(rank[:, :, :], greater[:, :, :, :], AX_X))

            def choose(i):
                dve.wait_ge(router_exped.sem, router_exped.at(i))
                step(i, 8, v.reduce_sum(exp_sum[:, :], exps[:, :, :], AX_X))
                step(i, 9, v.reciprocal(exp_inv[:, :], exp_sum[:, :]))
                step(i, 10, v.tensor_tensor(router_probs[:, :, :], exps[:, :, :],
                                         exp_inv[:, :].unsqueeze(2).to_broadcast(pair), ALU.mult))
                step(i, 11, v.scalar_tensor_tensor(out=coef[:, :, :], in0=rank[:, :, :], scalar=TOP_K - 0.5,
                                                in1=router_probs[:, :, :], op0=ALU.is_lt, op1=ALU.mult))

            def body(i, parity, active, steps):
                for z, kind, n in steps:
                    if z not in active:
                        continue
                    if kind == "moments":
                        measure(i, parity, z)
                    if kind == "normalise":
                        normalise(i, parity, z)
                    if kind == "norm_lo":
                        dve.wait_ge(xT_hi_done[z].sem, xT_hi_done[z].at(i))
                        remainder(xT_lo[z], gate_up_bank[1] if z == FFN else setup_bank,
                                  xT_hi[z]).then_inc(xT_lo_done[z].sem, 1)
                    if kind == "rotary_mul":
                        dve.wait_ge(rotary_projected.sem, rotary_projected.at(i, n + 1))
                        if isinstance(i, int) and i == 0 and n == 0:
                            dve.wait_ge(act_ready, 1)
                        if rotary_lo_done.begun(i, n):
                            dve.wait_ge(rotary_lo_done.sem, rotary_lo_done.at(i, n))
                        nc.vector.tensor_tensor(rotary_parts[:, :, :, :].rearrange("p a b t -> p a (b t)"),
                                                setup_bank[:, :].unsqueeze(1).to_broadcast([P, 2, 2 * T]),
                                                rotary_sb[:, :, :].rearrange("p (a b) t -> p a (b t)", b=2),
                                                ALU.mult).then_inc(rotary_multiplied.sem, 1)
                    if kind == "latent_moments":
                        dve.wait_ge(latent_projected.sem, latent_projected.at(i))
                        for s in range(NSEQ):
                            last = nc.vector.bn_stats(lat_stats[:, s, :], setup_bank[:, s * LATENT:(s + 1) * LATENT])
                        last.then_inc(latent_steps.sem, 1)
                        dve.wait_ge(latent_steps.sem, latent_steps.at(i, 1))
                        nc.vector.memset(wait_holder[:, :], 0.0)
                        for s in range(NSEQ):
                            last = nc.vector.bn_aggr(lat_moments[:, s, :], lat_stats[:, s, :])
                        last.then_inc(latent_steps.sem, 1)
                        dve.wait_ge(latent_steps.sem, latent_steps.at(i, 2))
                        nc.vector.tensor_scalar(lat_variance[:, :], lat_moments[:, :, 1], 1.0 / (WS * WS), EPS,
                                                ALU.mult, ALU.add).then_inc(latent_steps.sem, 1)
                    if kind == "latent_normalise":
                        dve.wait_ge(latent_rstd.sem, latent_rstd.at(i))
                        for s in range(NSEQ):
                            for k in range(2):
                                last = nc.vector.tensor_scalar(
                                    lat_twice[:, s, k, :], setup_bank[:, s * LATENT:(s + 1) * LATENT],
                                    lat_moments[:, s, 0:1], lat_rstd[:, s:s + 1], ALU.subtract, ALU.mult)
                        last.then_inc(latent_normed.sem, 1)
                    if kind == "latent_lo":
                        dve.wait_ge(latent_hi_done.sem, latent_hi_done.at(i))
                        nc.vector.tensor_tensor(latT_split[LATENT:P, :], latT[LATENT:P, :],
                                                latT_split[LATENT:P, :], ALU.subtract).then_inc(latent_split.sem, 1)
                    if kind in ("keys_lo", "queries_lo"):
                        m0, bias, k = (2, b2_scaled, 1) if kind == "keys_lo" else (0, b1_scaled, 2)
                        dve.wait_ge(qk_hi_done.sem, qk_hi_done.at(i, k))
                        if kind == "keys_lo":
                            if qk_stored[CROSS_OUT].begun(i - 1):
                                dve.wait_ge(qk_stored[CROSS_OUT].sem, qk_stored[CROSS_OUT].at(i - 1))
                        for m in range(KT):
                            last = nc.vector.scalar_tensor_tensor(
                                out=cross_qk_lo[:, m0 + m, :], in0=setup_bank[:, m * T:(m + 1) * T],
                                scalar=bias[:, m:m + 1], in1=cross_qk_hi[:, m0 + m, :],
                                op0=ALU.add, op1=ALU.subtract)
                        last.then_inc(qk_lo_done.sem, 1)
                    if kind == "values_add":
                        dve.wait_ge(values_projected[CROSS_OUT].sem, values_projected[CROSS_OUT].at(i))
                        if isinstance(i, int) and i == CROSS_IN:
                            dve.wait_ge(padding_ready, 4)
                        h = slot_of(parity, CROSS_IN)
                        for s in range(NSEQ):
                            last = nc.vector.scalar_tensor_tensor(
                                out=values[CROSS_OUT][h][:, s, :, 0:HD],
                                in0=setup_bank[:, s * D:(s + 1) * D].rearrange("p (h d) -> p h d", h=HEADS),
                                scalar=1.0 / WS, in1=b3_sb[:, :].rearrange("p (h d) -> p h d", h=HEADS),
                                op0=ALU.mult, op1=ALU.add)
                        last.then_inc(values_ready[CROSS_OUT].sem, 1)
                    if kind == "top":
                        dve.wait_ge(scored[z].sem, scored[z].at(i, n + 1))
                        s, g = divmod(n, GROUPS)
                        if z == SELF_OUT:
                            nc.vector.memset(wait_holder[:, :], 0.0)
                            for k in range(HG):
                                head = g * HG + k
                                last = nc.vector.tensor_tensor_reduce(
                                    masked_scores[:, k, :], score_bank[z][:, k * SEQ:(k + 1) * SEQ], causal_sb[:, :],
                                    1.0, LOWEST, ALU.add, ALU.max, top_score[z][:, s, head:head + 1])
                            last.then_inc(maxed[z].sem, 1)
                            continue
                        nc.vector.reduce_max(top_score[z][:, s, g * HG:(g + 1) * HG],
                                             score_bank[z][:, :].rearrange("p (h k) -> p h k", h=HG),
                                             AX_X).then_inc(maxed[z].sem, 1)
                    if kind == "divide":
                        dve.wait_ge(out_turned[z].sem, out_turned[z].at(i, n + 1))
                        summed = out_bank[z][:, :].rearrange("p (g h w) -> p g h w", g=GROUPS, w=VW)
                        inv = inverse[z][:, :].rearrange("p (g h) -> p g h", g=GROUPS)
                        nc.vector.reciprocal(inv, summed[:, :, :, HD]).then_inc(inverted[z].sem, 1)
                        dve.wait_ge(inverted[z].sem, inverted[z].at(i, n + 1))
                        heads = heads_out[z][:, n, :].rearrange("p (h d) -> p h d", d=HD)
                        nc.vector.tensor_tensor(
                            heads, out_bank[z][:, :].rearrange("p (h w) -> p h w", w=VW)[:, :, 0:HD],
                            inverse[z][:, :].unsqueeze(2).to_broadcast([P, HEADS, HD]),
                            ALU.mult).then_inc(divided[z].sem, 1)
                    if kind == "feature_lo":
                        dve.wait_ge(heads_hi_done[z].sem, heads_hi_done[z].at(i))
                        remainder(headsT_lo[z], out_bank[z], headsT_hi[z]).then_inc(heads_lo_done[z].sem, 1)
                    if kind == "residual":
                        dve.wait_ge(projected[z].sem, projected[z].at(i))
                        h = slot_of(parity, z)
                        if z == SELF_OUT:
                            dve.wait_ge(x_again_loaded.sem, x_again_loaded.at(i))
                            if x1_b4_done.begun(i - 1):
                                dve.wait_ge(x1_b4_done.sem, x1_b4_done.at(i - 1))
                            dst, src = x1[h], x_again
                        else:
                            if x1_b4_done.begun(i - 1):
                                dve.wait_ge(x1_b4_done.sem, x1_b4_done.at(i - 1))
                            if result_done.begun(i - 1):
                                dve.wait_ge(result_done.sem, result_done.at(i - 1))
                            dst, src = x2[h], x1_b4[h]
                        nc.vector.scalar_tensor_tensor(
                            out=dst[:, :, :].rearrange("p s d -> p (s d)"), in0=out_bank[z][:, :], scalar=1.0 / WS,
                            in1=src[:, :, :].rearrange("p s d -> p (s d)"), op0=ALU.mult,
                            op1=ALU.add).then_inc(residual_added[z].sem, 1)
                    if kind == "rank":
                        rank_experts(i)
                    if kind == "choose":
                        choose(i)
                    if kind == "product":
                        dve.wait_ge(tanh_done.sem, tanh_done.at(i, n + 1))
                        if hidden_done.begun(i, n):
                            dve.wait_ge(hidden_done.sem, hidden_done.at(i, n))
                        nc.vector.scalar_tensor_tensor(out=gated[:, :], in0=tanh_sb[:, :], scalar=1.0,
                                                       in1=gate_up_bank[n % 2][:, 0:T], op0=ALU.add,
                                                       op1=ALU.mult).then_inc(gated_done.sem, 1)
                        dve.wait_ge(gated_done.sem, gated_done.at(i, n + 1))
                        if hidden_lo_done.begun(i, n - 1):
                            dve.wait_ge(hidden_lo_done.sem, hidden_lo_done.at(i, n - 1))
                        if n > SHARED_TILES:
                            if hidden_scaled.begun(i, n - SHARED_TILES):
                                dve.wait_ge(hidden_scaled.sem, hidden_scaled.at(i, n - SHARED_TILES))
                        dst = hidden_c[:, n % 2, :] if n < SHARED_TILES else hidden[:, :]
                        nc.vector.scalar_tensor_tensor(out=dst, in0=gate_up_bank[n % 2][:, T:2 * T], scalar=0.5 / WS,
                                                       in1=gated[:, :], op0=ALU.mult,
                                                       op1=ALU.mult).then_inc(hidden_done.sem, 1)
                        if n >= SHARED_TILES:
                            e = n - SHARED_TILES
                            dve.wait_ge(hidden_done.sem, hidden_done.at(i, n + 1))
                            dve.wait_ge(coef_spread[e % 2].sem, coef_spread[e % 2].at(i, e // 2 + 1))
                            nc.vector.tensor_tensor(hidden_c[:, n % 2, :], hidden[:, :], coef_rows[:, e % 2, :],
                                                    ALU.mult).then_inc(hidden_scaled.sem, 1)
                    if kind == "result":
                        dve.wait_ge(down_done.sem, down_done.at(i))
                        if result_stored.begun(i - 1):
                            dve.wait_ge(result_stored.sem, result_stored.at(i - 1))
                        nc.vector.scalar_tensor_tensor(
                            out=result[:, :, :].rearrange("p s d -> p (s d)"), in0=down_bank[:, :],
                            scalar=1.0 / (WS * WS), in1=x2[slot_of(parity, FFN)][:, :, :].rearrange("p s d -> p (s d)"),
                            op0=ALU.mult, op1=ALU.add).then_inc(result_done.sem, 1)

            run(dve, body, lambda: split_remainders(FIRST_CHUNKS, len(chunks)))

        @block.tensor
        def _(pe):
            mm = nc.tensor.matmul
            pe.wait_ge(chunk_lo, FIRST_CHUNKS)
            pe.wait_ge(act_ready, 1)
            pe.wait_ge(pool_ready, 1)

            def split_product(dst, pairs, opened=False, closes=True):
                n = 0
                for (lh, ll), (rh, rl) in pairs:
                    for a, b in ((lh, rh), (lh, rl), (ll, rh)):
                        n += 1
                        last = mm(dst, a, b, start=(n == 1 and not opened),
                                  stop=(closes and n == 3 * len(pairs)), skip_group_check=True)
                return last

            def turn(dst_bank, src):
                for kt in range(KT):
                    for s in range(NSEQ):
                        c = (kt * NSEQ + s) * SEQ
                        last = nc.tensor.transpose(dst_bank[:, c:c + SEQ], src[:, s, kt * P:(kt + 1) * P], ident[:, :])
                return last

            def setup_free(i, active, z):
                if z == SELF_IN:
                    if values_ready[SELF_OUT].begun(i - 1):
                        pe.wait_ge(values_ready[SELF_OUT].sem, values_ready[SELF_OUT].at(i - 1))
                    if not isinstance(i, int) or i - 1 >= CROSS_IN:
                        if values_ready[CROSS_OUT].begun(i - 1):
                            pe.wait_ge(values_ready[CROSS_OUT].sem, values_ready[CROSS_OUT].at(i - 1))
                else:
                    if values_ready[CROSS_OUT].begun(i - 1):
                        pe.wait_ge(values_ready[CROSS_OUT].sem, values_ready[CROSS_OUT].at(i - 1))
                    if SELF_IN in active:
                        pe.wait_ge(values_ready[SELF_OUT].sem, values_ready[SELF_OUT].at(i))

            def tokens(hi, lo, kt, s):
                a = slice(s * SEQ, (s + 1) * SEQ)
                return hi[:, kt, a], lo[:, kt, a]

            def body(i, parity, active, steps):
                for z, kind, n in steps:
                    if z not in active:
                        continue
                    if kind == "norm_turn":
                        pe.wait_ge(norm_done[z].sem, norm_done[z].at(i))
                        if z == FFN:
                            if hidden_done.begun(i - 1):
                                pe.wait_ge(hidden_done.sem, hidden_done.at(i - 1))
                            turn(gate_up_bank[1], normed[z]).then_inc(norm_turned[z].sem, 1)
                        else:
                            if z == SELF_IN:
                                setup_free(i, active, z)
                            else:
                                pe.wait_ge(qk_lo_done.sem, qk_lo_done.at(i, 1))
                            turn(setup_bank, normed[z]).then_inc(norm_turned[z].sem, 1)
                    if kind == "rotary":
                        if n == 0:
                            pe.wait_ge(xT_lo_done[SELF_IN].sem, xT_lo_done[SELF_IN].at(i))
                        if n == 1:
                            pe.wait_ge(latent_split.sem, latent_split.at(i))
                        for half in range(2):
                            dst = setup_bank[:, half * T:(half + 1) * T]
                            if n == 0:
                                last = split_product(dst, [(w("q", kt, half * P, P), (xT_hi[SELF_IN][:, kt, :],
                                                                                     xT_lo[SELF_IN][:, kt, :]))
                                                           for kt in range(KT)])
                            else:
                                a = LAT["k"] + half * P
                                mm(dst, lat_hi[:, a:a + P], latT_split[:, :], start=True, stop=False)
                                last = mm(dst, lat_lo[:, a:a + P], latT_split[:, :], start=False, stop=True)
                        last.then_inc(rotary_projected.sem, 1)
                    if kind == "latent":
                        pe.wait_ge(rotary_multiplied.sem, rotary_multiplied.at(i, 1))
                        for s in range(NSEQ):
                            last = split_product(setup_bank[:, s * LATENT:(s + 1) * LATENT],
                                                 [(tokens(xT_hi[SELF_IN], xT_lo[SELF_IN], kt, s),
                                                   w("down_latent", kt, 0, LATENT)) for kt in range(KT)])
                        last.then_inc(latent_projected.sem, 1)
                    if kind == "latent_turn":
                        pe.wait_ge(latent_normed.sem, latent_normed.at(i))
                        for s in range(NSEQ):
                            last = nc.tensor.transpose(setup_bank[:, s * SEQ:(s + 1) * SEQ],
                                                       lat_twice[:, s, :, :].rearrange("p a l -> p (a l)"), ident[:, :])
                        last.then_inc(latent_turned.sem, 1)
                    if kind == "latent_values":
                        pe.wait_ge(rotary_multiplied.sem, rotary_multiplied.at(i))
                        for s in range(NSEQ):
                            dst = setup_bank[:, s * D:(s + 1) * D]
                            lat = latT_split[:, s * SEQ:(s + 1) * SEQ]
                            mm(dst, lat, lat_hi[:, LAT["v"]:LAT["v"] + D], start=True, stop=False)
                            last = mm(dst, lat, lat_lo[:, LAT["v"]:LAT["v"] + D], start=False, stop=True)
                        last.then_inc(values_projected[SELF_OUT].sem, 1)
                    if kind in ("keys", "queries"):
                        if kind == "keys":
                            pe.wait_ge(ctx_lo_done.sem, ctx_lo_done.at(i))
                            setup_free(i, active, z)
                            name, hi, lo = "cross_k", ctxT_hi, ctxT_lo
                        else:
                            pe.wait_ge(xT_lo_done[CROSS_IN].sem, xT_lo_done[CROSS_IN].at(i))
                            name, hi, lo = "cross_q", xT_hi[CROSS_IN], xT_lo[CROSS_IN]
                        for m in range(KT):
                            last = split_product(setup_bank[:, m * T:(m + 1) * T],
                                                 [(w(name, kt, m * P, P), (hi[:, kt, :], lo[:, kt, :]))
                                                  for kt in range(KT)])
                        last.then_inc(qk_projected.sem, 1)
                    if kind == "context_values":
                        pe.wait_ge(qk_lo_done.sem, qk_lo_done.at(i, 2))
                        for s in range(NSEQ):
                            last = split_product(setup_bank[:, s * D:(s + 1) * D],
                                                 [(tokens(ctxT_hi, ctxT_lo, kt, s), w("cross_v", kt, 0, D))
                                                  for kt in range(KT)])
                        last.then_inc(values_projected[CROSS_OUT].sem, 1)
                    if kind in ("scores", "weights"):
                        s, g = divmod(n, GROUPS)
                        h = slot_of(parity, z)
                        a = slice(s * SEQ, (s + 1) * SEQ)
                        if kind == "scores":
                            if n == 0:
                                if qk_packed[z].begun(i - 1):
                                    pe.wait_ge(qk_packed[z].sem, qk_packed[z].at(i - 1))
                            if g == 0:
                                if exped[z].begun(i, s * GROUPS):
                                    pe.wait_ge(exped[z].sem, exped[z].at(i, s * GROUPS))
                            else:
                                if maxed[z].begun(i, n):
                                    pe.wait_ge(maxed[z].sem, maxed[z].at(i, n))
                        else:
                            if g == 0:
                                pe.wait_ge(maxed[z].sem, maxed[z].at(i, (s + 1) * GROUPS))
                            else:
                                if exped[z].begun(i, n):
                                    pe.wait_ge(exped[z].sem, exped[z].at(i, n))
                            if z == SELF_OUT:
                                pe.wait_ge(top_masked_done.sem, top_masked_done.at(i, n + 1))
                        for k in range(HG):
                            head = g * HG + k
                            dst = score_bank[z][:, k * SEQ:(k + 1) * SEQ]
                            q = q_packed[z][h][:, head, a]
                            keys = k_packed[z][h][:, head // 2, a]
                            if kind == "scores":
                                last = mm(dst, q, keys, start=True, stop=True, skip_group_check=True)
                            else:
                                mm(dst, keys, q, start=True, stop=False, skip_group_check=True)
                                if z == SELF_OUT:
                                    top = top_masked[:, head, :]
                                else:
                                    top = top_score[z][:, s, head:head + 1].to_broadcast([P, P])
                                last = mm(dst, top, minus_ident[:, :], start=False, stop=True, skip_group_check=True)
                        last.then_inc((scored if kind == "scores" else weighed)[z].sem, 1)
                    if kind == "values":
                        s, g = divmod(n, GROUPS)
                        pe.wait_ge(exped[z].sem, exped[z].at(i, n + 1))
                        if n == 0:
                            if values_ready[z].begun(i - 1):
                                pe.wait_ge(values_ready[z].sem, values_ready[z].at(i - 1))
                            if residual_added[z].begun(i - 1):
                                pe.wait_ge(residual_added[z].sem, residual_added[z].at(i - 1))
                        if n == GROUPS:
                            pe.wait_ge(divided[z].sem, divided[z].at(i, 1))
                        for k in range(HG):
                            head = g * HG + k
                            last = mm(out_bank[z][VW * k:VW * (k + 1), g * SEQ:(g + 1) * SEQ],
                                      values[z][slot_of(parity, z)][:, s, head, :], probs[z][:, head, :],
                                      start=True, stop=True, tile_position=(0, VW * k), skip_group_check=True)
                        last.then_inc(valued[z].sem, 1)
                    if kind == "out_turn":
                        pe.wait_ge(out_copied[z].sem, out_copied[z].at(i, n + 1))
                        for g in range(GROUPS):
                            last = nc.tensor.transpose(out_bank[z][:, g * SEQ:(g + 1) * SEQ],
                                                       outT[z][:, g * SEQ:(g + 1) * SEQ], ident[:, :])
                        last.then_inc(out_turned[z].sem, 1)
                    if kind == "feature_turn":
                        pe.wait_ge(divided[z].sem, divided[z].at(i))
                        turn(out_bank[z], heads_out[z]).then_inc(heads_turned[z].sem, 1)
                    if kind == "project":
                        pe.wait_ge(heads_lo_done[z].sem, heads_lo_done[z].at(i))
                        name = "self_out" if z == SELF_OUT else "cross_out"
                        for s in range(NSEQ):
                            last = split_product(out_bank[z][:, s * D:(s + 1) * D],
                                                 [(tokens(headsT_hi[z], headsT_lo[z], kt, s), w(name, kt, 0, D))
                                                  for kt in range(KT)])
                        last.then_inc(projected[z].sem, 1)
                    if kind == "router":
                        pe.wait_ge(xT_lo_done[FFN].sem, xT_lo_done[FFN].at(i))
                        for s in range(NSEQ):
                            last = split_product(gate_up_bank[1][:, s * EXPERTS:(s + 1) * EXPERTS],
                                                 [(tokens(xT_hi[FFN], xT_lo[FFN], kt, s), w("router", kt, 0, EXPERTS))
                                                  for kt in range(KT)])
                        last.then_inc(routed.sem, 1)
                    if kind in ("gate", "up"):
                        if kind == "gate":
                            if n == 0:
                                pe.wait_ge(xT_lo_done[FFN].sem, xT_lo_done[FFN].at(i))
                            if n == 1:
                                pe.wait_ge(coef_copied.sem, coef_copied.at(i))
                            if hidden_done.begun(i, n - 1):
                                pe.wait_ge(hidden_done.sem, hidden_done.at(i, n - 1))
                        half = int(kind == "up")
                        name, c = ("shared_" + kind, n * P) if n < SHARED_TILES else (kind, (n - SHARED_TILES) * P)
                        last = split_product(gate_up_bank[n % 2][:, half * T:(half + 1) * T],
                                             [(w(name, kt, c, P), (xT_hi[FFN][:, kt, :], xT_lo[FFN][:, kt, :]))
                                              for kt in range(KT)])
                        if kind == "up":
                            last.then_inc(gate_up_done.sem, 1)
                    if kind == "coef_turn":
                        pe.wait_ge(choose_steps.sem, choose_steps.at(i))
                        nc.tensor.transpose(gate_up_bank[1][0:NSEQ * EXPERTS, 0:SEQ],
                                            coef[:, :, :].rearrange("p s e -> p (s e)"),
                                            ident[:, :]).then_inc(coef_turned.sem, 1)
                    if kind == "down":
                        if n == 0:
                            if result_done.begun(i - 1):
                                pe.wait_ge(result_done.sem, result_done.at(i - 1))
                        pe.wait_ge(hidden_lo_done.sem, hidden_lo_done.at(i, n + 1))
                        if n < SHARED_TILES:
                            weights = w("shared_down", n, 0, D)
                        else:
                            c = (n - SHARED_TILES) * D
                            weights = down_hi[:, c:c + D], down_lo[:, c:c + D]
                        for s in range(NSEQ):
                            a = slice(s * SEQ, (s + 1) * SEQ)
                            last = split_product(down_bank[:, s * D:(s + 1) * D],
                                                 [((hidden_hi[:, n % 2, a], hidden_lo[:, n % 2, a]), weights)],
                                                 opened=not (n == 0 and s == 0), closes=n == TILES - 1)
                        last.then_inc(down_done.sem, 1)

            run(pe, body, lambda: pe.wait_ge(chunk_lo, len(chunks)))


def _layout(a):
    f = np.float32
    halves = np.arange(D).reshape(HEADS, 2, HD // 2).transpose(1, 0, 2).reshape(-1)
    wide = np.concatenate([
        a["L0_attn_W_q"][:, halves], a["L0_attn_W_dkv"], a["L0_attn_W_o"],
        a["L0_xattn_w1"].T, a["L0_xattn_w2"].T, a["L0_xattn_w3"].T, a["L0_xattn_w4"].T,
        a["L0_ffn_shared_gate"], a["L0_ffn_shared_up"], a["L0_ffn_shared_down"], a["L0_ffn_router"],
        a["L0_ffn_experts_gate"].transpose(1, 0, 2).reshape(D, EXPERTS * P),
        a["L0_ffn_experts_up"].transpose(1, 0, 2).reshape(D, EXPERTS * P)], axis=1)
    expert_down = a["L0_ffn_experts_down"].transpose(1, 0, 2).reshape(P, EXPERTS * D)
    lat = np.concatenate([a["L0_attn_W_uk"][:, halves], a["L0_attn_W_uv"]], axis=1)
    lat = np.concatenate([lat, lat], axis=0)
    twice = lambda v: np.concatenate([v, v]).reshape(P, 1)
    rows = lambda v: np.broadcast_to(v.reshape(1, D), (P, D))
    half = HD // 2
    inv_freq = f(1.0) / f(10000.0) ** (np.arange(half, dtype=f) / f(half))
    angles = np.arange(SEQ, dtype=f)[:, None] * inv_freq[None, :]
    cos, sin = np.cos(angles).astype(f).T, np.sin(angles).astype(f).T
    cos, sin = np.tile(cos, (HEADS, NSEQ)), np.tile(sin, (HEADS, NSEQ))
    t = np.arange(SEQ)
    causal = np.where(t[None, :] > t[:, None], f(MASKED), f(0)).astype(f)
    return {"x": a["x"], "ctxT": a["ctx_1024"].transpose(0, 2, 1), "wide": wide,
            "expert_down": expert_down, "latent_weights": lat,
            "gamma": twice(a["L0_attn_ln_gamma"]), "beta": twice(a["L0_attn_ln_beta"]),
            "b1": a["L0_xattn_b1"].reshape(KT, P).T, "b2": a["L0_xattn_b2"].reshape(KT, P).T,
            "b3": rows(a["L0_xattn_b3"]), "b4": rows(a["L0_xattn_b4"]),
            "rotary_table": np.concatenate([cos, -sin, sin, cos], axis=1), "causal": causal}


def kernel(**inputs):
    import concourse.bacc as _bacc
    from concourse.bass_utils import run_bass_kernel_spmd as _run

    nc = _bacc.Bacc("TRN2", target_bir_lowering=False, num_devices=1)
    arrays, args = {}, []
    for name, a in _layout({k: np.asarray(v) for k, v in inputs.items()}).items():
        a = np.ascontiguousarray(a)
        arrays[f"in_{name}"] = a
        args.append(nc.dram_tensor(f"in_{name}", a.shape, mybir.dt.from_np(a.dtype), kind="ExternalInput").ap())
    out = nc.dram_tensor("out_x", (BATCH, SEQ, D), F32, kind="ExternalOutput").ap()
    decoder_layer(nc, *args, out)
    r = _run(nc, [arrays], core_ids=[0])
    return r.results[0]["out_x"]
```
